# Optimizing a Trainium2 kernel written in Bass

```python
import numpy as np
import jax
import jax.numpy as jnp

def _softmax(x, axis=-1):
    return jax.nn.softmax(x, axis=axis)

def _gelu(x):
    return jax.nn.gelu(x, approximate=True)

def _silu(x):
    return jax.nn.silu(x)

def _sigmoid(x):
    return jax.nn.sigmoid(x)

def _layernorm(x, axis=-1, eps=1e-05):
    m = jnp.mean(x, axis=axis, keepdims=True)
    v = jnp.var(x, axis=axis, keepdims=True)
    return (x - m) / jnp.sqrt(v + eps)

def _scatter_add(tgt, idx, src, axis=0):
    return tgt.at[idx].add(src)

def _segment_sum(src, seg, n):
    return jax.ops.segment_sum(src, seg, n)
kernel_name = 'mk_conv_attn_hybrid_d2_conv_nchw384_r2_3d1904'

def setup_inputs(seed: int=0):
    np.random.seed(seed)
    _w = jnp.asarray

    def _rec_inputs():
        import jax
        import jax.numpy as jnp
        _gk = jax.random.key(seed)
        x = -0.0002221 + 1 * jax.random.normal(jax.random.fold_in(_gk, 1), (16, 192, 32, 32), jnp.float32)
        return x
    x = _rec_inputs()

    def _L0_conv_setup():
        import jax, jax.numpy as jnp
        import numpy as np
        B, C, S, NH = (16, 192, 32, 8)
        HC = C // NH
        EPS = 1e-05

        def _dwconv(x, w, b):
            y = jax.lax.conv_general_dilated(x, w, window_strides=(1, 1), padding='SAME', feature_group_count=x.shape[1], dimension_numbers=('NCHW', 'OIHW', 'NCHW'))
            return y + b[None, :, None, None]

        def _proj(xn, wp, bp, wd, bd):
            b_, c_, s1, s2 = xn.shape
            xh = xn.reshape(b_, NH, HC, s1, s2)
            y = jnp.einsum('bhcij,hoc->bhoij', xh, wp) + bp[None, :, :, None, None]
            y = _dwconv(y.reshape(b_, c_, s1, s2), wd, bd).reshape(b_, NH, HC, s1, s2)
            return jnp.transpose(y, (0, 1, 4, 3, 2)).reshape(b_, NH, s2 * s1, HC)
        key = jax.random.key(seed)
        ks = jax.random.split(key, 10)
        sc = 0.05
        n = lambda k, shape: jax.random.normal(k, shape, jnp.float32) * sc
        return {'x': jax.random.normal(ks[0], (B, C, S, S), jnp.float32), 'ln_g': jnp.ones((C, S, S), jnp.float32), 'ln_b': jnp.zeros((C, S, S), jnp.float32), 'wq_p': n(ks[1], (NH, HC, HC)), 'bq_p': jnp.zeros((NH, HC), jnp.float32), 'wq_d': n(ks[2], (C, 1, 3, 3)), 'bq_d': jnp.zeros((C,), jnp.float32), 'wk_p': n(ks[3], (NH, HC, HC)), 'bk_p': jnp.zeros((NH, HC), jnp.float32), 'wk_d': n(ks[4], (C, 1, 3, 3)), 'bk_d': jnp.zeros((C,), jnp.float32), 'wv_p': n(ks[5], (NH, HC, HC)), 'bv_p': jnp.zeros((NH, HC), jnp.float32), 'wv_d': n(ks[6], (C, 1, 3, 3)), 'bv_d': jnp.zeros((C,), jnp.float32), 'alpha': jnp.ones((NH,), jnp.float32), 'w_f': n(ks[7], (C, C)), 'b_f': jnp.zeros((C,), jnp.float32)}
    _L0_conv_all = _L0_conv_setup()
    _L0_conv_in = {k: v for k, v in _L0_conv_all.items() if k in ('ln_g', 'ln_b', 'wq_p', 'bq_p', 'wq_d', 'bq_d', 'wk_p', 'bk_p', 'wk_d', 'bk_d', 'wv_p', 'bv_p', 'wv_d', 'bv_d', 'alpha', 'w_f', 'b_f')}
    del _L0_conv_all

    def _L1_attn_setup():
        import jax, jax.numpy as jnp
        import numpy as np
        B, T, C = (64, 128, 192)
        H, HS = (6, 32)
        key = jax.random.key(seed)
        k1, k2, k3, k4 = jax.random.split(key, 4)
        scale_qkv = (1.0 / C) ** 0.5
        scale_proj = (1.0 / (H * HS)) ** 0.5
        return {'x': jax.random.normal(k1, (B, T, C), dtype=jnp.float32), 'W_qkv': jax.random.normal(k2, (3 * H * HS, C), dtype=jnp.float32) * scale_qkv, 'W_proj': jax.random.normal(k3, (C, H * HS), dtype=jnp.float32) * scale_proj, 'b_proj': jax.random.normal(k4, (C,), dtype=jnp.float32) * 0.01}
    _L1_attn_all = _L1_attn_setup()
    _L1_attn_in = {k: v for k, v in _L1_attn_all.items() if k in ('W_qkv', 'W_proj', 'b_proj')}
    del _L1_attn_all

    def _L1_ffn_setup():
        import jax, jax.numpy as jnp
        import numpy as np
        NUM_EXPERTS = 4
        TOP_K = 2
        DIM = 192
        HID = 4 * DIM
        key = jax.random.key(seed)
        ks = jax.random.split(key, 5)
        B, S = (16, 1024)
        scale_in = 1.0 / np.sqrt(DIM)
        scale_hid = 1.0 / np.sqrt(HID)
        return {'x': jax.random.normal(ks[0], (B, S, DIM), dtype=jnp.float32), 'gate_w': jax.random.normal(ks[1], (DIM, NUM_EXPERTS), dtype=jnp.float32) * scale_in, 'gate_b': jnp.zeros((NUM_EXPERTS,), dtype=jnp.float32), 'w1': jax.random.normal(ks[2], (NUM_EXPERTS, DIM, HID), dtype=jnp.float32) * scale_in, 'b1': jnp.zeros((NUM_EXPERTS, HID), dtype=jnp.float32), 'w2': jax.random.normal(ks[3], (NUM_EXPERTS, HID, DIM), dtype=jnp.float32) * scale_hid, 'b2': jnp.zeros((NUM_EXPERTS, DIM), dtype=jnp.float32)}
    _L1_ffn_all = _L1_ffn_setup()
    _L1_ffn_in = {k: v for k, v in _L1_ffn_all.items() if k in ('gate_w', 'gate_b', 'w1', 'b1', 'w2', 'b2')}
    del _L1_ffn_all
    return {'x': x, 'L0_conv_ln_g': _L0_conv_in['ln_g'], 'L0_conv_ln_b': _L0_conv_in['ln_b'], 'L0_conv_wq_p': _L0_conv_in['wq_p'], 'L0_conv_bq_p': _L0_conv_in['bq_p'], 'L0_conv_wq_d': _L0_conv_in['wq_d'], 'L0_conv_bq_d': _L0_conv_in['bq_d'], 'L0_conv_wk_p': _L0_conv_in['wk_p'], 'L0_conv_bk_p': _L0_conv_in['bk_p'], 'L0_conv_wk_d': _L0_conv_in['wk_d'], 'L0_conv_bk_d': _L0_conv_in['bk_d'], 'L0_conv_wv_p': _L0_conv_in['wv_p'], 'L0_conv_bv_p': _L0_conv_in['bv_p'], 'L0_conv_wv_d': _L0_conv_in['wv_d'], 'L0_conv_bv_d': _L0_conv_in['bv_d'], 'L0_conv_alpha': _L0_conv_in['alpha'], 'L0_conv_w_f': _L0_conv_in['w_f'], 'L0_conv_b_f': _L0_conv_in['b_f'], 'L1_attn_W_qkv': _L1_attn_in['W_qkv'], 'L1_attn_W_proj': _L1_attn_in['W_proj'], 'L1_attn_b_proj': _L1_attn_in['b_proj'], 'L1_ffn_gate_w': _L1_ffn_in['gate_w'], 'L1_ffn_gate_b': _L1_ffn_in['gate_b'], 'L1_ffn_w1': _L1_ffn_in['w1'], 'L1_ffn_b1': _L1_ffn_in['b1'], 'L1_ffn_w2': _L1_ffn_in['w2'], 'L1_ffn_b2': _L1_ffn_in['b2']}

def reference(x, L0_conv_ln_g, L0_conv_ln_b, L0_conv_wq_p, L0_conv_bq_p, L0_conv_wq_d, L0_conv_bq_d, L0_conv_wk_p, L0_conv_bk_p, L0_conv_wk_d, L0_conv_bk_d, L0_conv_wv_p, L0_conv_bv_p, L0_conv_wv_d, L0_conv_bv_d, L0_conv_alpha, L0_conv_w_f, L0_conv_b_f, L1_attn_W_qkv, L1_attn_W_proj, L1_attn_b_proj, L1_ffn_gate_w, L1_ffn_gate_b, L1_ffn_w1, L1_ffn_b1, L1_ffn_w2, L1_ffn_b2):
    import jax
    import jax.numpy as jnp

    def _L0_conv_ref(x, ln_g, ln_b, wq_p, bq_p, wq_d, bq_d, wk_p, bk_p, wk_d, bk_d, wv_p, bv_p, wv_d, bv_d, alpha, w_f, b_f):
        import jax, jax.numpy as jnp
        import numpy as np
        B, C, S, NH = (16, 192, 32, 8)
        HC = C // NH
        EPS = 1e-05

        def _dwconv(x, w, b):
            y = jax.lax.conv_general_dilated(x, w, window_strides=(1, 1), padding='SAME', feature_group_count=x.shape[1], dimension_numbers=('NCHW', 'OIHW', 'NCHW'))
            return y + b[None, :, None, None]

        def _proj(xn, wp, bp, wd, bd):
            b_, c_, s1, s2 = xn.shape
            xh = xn.reshape(b_, NH, HC, s1, s2)
            y = jnp.einsum('bhcij,hoc->bhoij', xh, wp) + bp[None, :, :, None, None]
            y = _dwconv(y.reshape(b_, c_, s1, s2), wd, bd).reshape(b_, NH, HC, s1, s2)
            return jnp.transpose(y, (0, 1, 4, 3, 2)).reshape(b_, NH, s2 * s1, HC)
        mu = jnp.mean(x, axis=(1, 2, 3), keepdims=True)
        var = jnp.mean((x - mu) ** 2, axis=(1, 2, 3), keepdims=True)
        xn = (x - mu) * jax.lax.rsqrt(var + EPS) * ln_g + ln_b
        Q = _proj(xn, wq_p, bq_p, wq_d, bq_d)
        K = _proj(xn, wk_p, bk_p, wk_d, bk_d)
        V = _proj(xn, wv_p, bv_p, wv_d, bv_d)
        logits = jnp.einsum('bhnc,bhnd->bhcd', K, Q) / alpha[None, :, None, None]
        attn = jax.nn.softmax(logits, axis=-1)
        out = jnp.einsum('bhnc,bhcd->bhnd', V, attn)
        b_, _, _, s = x.shape
        out = out.reshape(b_, NH, s, s, HC)
        out = jnp.transpose(out, (0, 1, 4, 3, 2)).reshape(b_, C, s, s)
        return jnp.einsum('bcij,oc->boij', out, w_f) + b_f[None, :, None, None] + xn

    def _L1_attn_ref(x, W_qkv, W_proj, b_proj):
        import jax, jax.numpy as jnp
        import numpy as np
        B, T, C = (64, 128, 192)
        H, HS = (6, 32)
        Bq, Tq, Cq = x.shape
        qkv = jnp.einsum('btc,fc->btf', x, W_qkv)
        qkv = qkv.reshape(Bq, Tq, H, 3, HS)
        k = qkv[..., 0, :]
        q = qkv[..., 1, :]
        v = qkv[..., 2, :]
        scale = HS ** (-0.5)
        wei = jnp.einsum('bqhd,bkhd->bhqk', q, k) * scale
        causal = jnp.tril(jnp.ones((Tq, Tq), dtype=bool))
        wei = jnp.where(causal[None, None], wei, -jnp.inf)
        wei = jax.nn.softmax(wei, axis=-1)
        out = jnp.einsum('bhqk,bkhd->bqhd', wei, v).reshape(Bq, Tq, H * HS)
        out = jnp.einsum('btf,cf->btc', out, W_proj) + b_proj
        out = jnp.einsum('btf,cf->btc', out, W_proj) + b_proj
        return out

    def _L1_ffn_ref(x, gate_w, gate_b, w1, b1, w2, b2):
        import jax, jax.numpy as jnp
        import numpy as np
        NUM_EXPERTS = 4
        TOP_K = 2
        DIM = 192
        HID = 4 * DIM
        scores = jnp.einsum('bsd,de->bse', x, gate_w) + gate_b
        probs = jax.nn.softmax(scores, axis=-1)
        topk_vals, topk_idx = jax.lax.top_k(probs, TOP_K)
        mask = jnp.sum(jax.nn.one_hot(topk_idx, NUM_EXPERTS, dtype=probs.dtype), axis=-2)
        masked = probs * mask
        masked = masked / (jnp.sum(masked, axis=-1, keepdims=True) + 1e-09)
        h = jax.nn.gelu(jnp.einsum('bsd,edh->ebsh', x, w1) + b1[:, None, None, :], approximate=False)
        y = jnp.einsum('ebsh,ehd->ebsd', h, w2) + b2[:, None, None, :]
        out = jnp.einsum('bse,ebsd->bsd', masked, y)
        return out

    def _gn(v, G=32, eps=1e-05):
        B_, C_, H_, W_ = v.shape
        g = v.reshape(B_, G, C_ // G, H_, W_)
        m = jnp.mean(g, axis=(2, 3, 4), keepdims=True)
        s = jnp.var(g, axis=(2, 3, 4), keepdims=True)
        return ((g - m) / jnp.sqrt(s + eps)).reshape(v.shape)

    def _ln_c(v, eps=1e-06):
        m = jnp.mean(v, axis=1, keepdims=True)
        s = jnp.var(v, axis=1, keepdims=True)
        return (v - m) / jnp.sqrt(s + eps)

    def _ln_t(v, eps=1e-05):
        m = jnp.mean(v, axis=-1, keepdims=True)
        s = jnp.var(v, axis=-1, keepdims=True)
        return (v - m) / jnp.sqrt(s + eps)

    def _to_tokens(v):
        B_, C_, H_, W_ = v.shape
        return v.reshape(B_, C_, H_ * W_).transpose(0, 2, 1)

    def _from_tokens(t, like):
        B_, C_, H_, W_ = like.shape
        return t.transpose(0, 2, 1).reshape(B_, C_, H_, W_)
    x = _L0_conv_ref(x, L0_conv_ln_g, L0_conv_ln_b, L0_conv_wq_p, L0_conv_bq_p, L0_conv_wq_d, L0_conv_bq_d, L0_conv_wk_p, L0_conv_bk_p, L0_conv_wk_d, L0_conv_bk_d, L0_conv_wv_p, L0_conv_bv_p, L0_conv_wv_d, L0_conv_bv_d, L0_conv_alpha, L0_conv_w_f, L0_conv_b_f)
    t = _to_tokens(x)
    t = t + _L1_attn_ref(_ln_t(t), L1_attn_W_qkv, L1_attn_W_proj, L1_attn_b_proj)
    t = t + _L1_ffn_ref(_ln_t(t), L1_ffn_gate_w, L1_ffn_gate_b, L1_ffn_w1, L1_ffn_b1, L1_ffn_w2, L1_ffn_b2)
    x = _from_tokens(t, x)
    return x

_drawn_inputs = setup_inputs


def setup_inputs(seed=0):
    import zlib

    import numpy as np

    out = dict(_drawn_inputs(seed))
    spreads = {'L0_conv_ln_g': (1.0, 0.2),
     'L0_conv_ln_b': (0.0, 0.1),
     'L0_conv_bq_p': (0.0, 0.1),
     'L0_conv_bq_d': (0.0, 0.1),
     'L0_conv_bk_p': (0.0, 0.1),
     'L0_conv_bk_d': (0.0, 0.1),
     'L0_conv_bv_p': (0.0, 0.1),
     'L0_conv_bv_d': (0.0, 0.1),
     'L0_conv_alpha': (1.0, 0.6),
     'L0_conv_b_f': (0.0, 0.1),
     'L1_ffn_gate_b': (0.0, 0.1),
     'L1_ffn_b1': (0.0, 0.1),
     'L1_ffn_b2': (0.0, 0.1)}
    factors = {'L0_conv_wq_p': 3.902, 'L0_conv_wk_p': 5.529}
    for name, (base, spread) in spreads.items():
        noise = np.random.default_rng([zlib.crc32(name.encode()), seed]).standard_normal(out[name].shape)
        drawn = base * np.exp(spread * noise) if base else spread * noise
        out[name] = jnp.asarray(drawn.astype(out[name].dtype))
    for name, factor in factors.items():
        out[name] = (out[name] * factor).astype(out[name].dtype)
    return out
```

```python
from contextlib import ExitStack

import concourse.bass as bass
from concourse import mybir

F32 = mybir.dt.float32
F32R = mybir.dt.float32r
BF16 = mybir.dt.bfloat16
ALU = mybir.AluOpType
ACT = mybir.ActivationFunctionType
AX = mybir.AxisListType.X

NEG = -3.0e38
P = 128
BANK = 512


def hybrid_block_kernel(nc, x, ln_g, ln_b, conv_w, conv_bias_row, conv_taps, conv_bias, alpha_rows, w_f_t, b_f,
                        w_qkv_a, w_qkv_b, w_proj, w_proj_t, b_proj, gate_w_a, gate_w_b, gate_b, w1_a, w1_b, b1_t,
                        w2, b2, out):
    B, C, SH, SW = x.shape
    N = SH * SW
    NC = N // P
    HALF = C // 2
    NH, HC = conv_w.shape[1], conv_w.shape[0]
    HPH = NH // 2
    CM = conv_w.shape[2]
    PW = SW + 2
    XP = 1160
    SL = SH * PW
    TAPS = [3 * dy + dx for dy in range(3) for dx in range(3)]
    SHIFT = [PW * dy + dx for dy in range(3) for dx in range(3)]
    STACKS = [TAPS[:5], TAPS[5:]]
    KROWS = [(HC + 1) * len(s) for s in STACKS]
    H, D = 6, C // 6
    GROUPS = [[0, 1, 2, 3], [4, 5]]
    SCALE = float(D) ** -0.5
    E = gate_w_a.shape[1]
    HID = w1_a.shape[1] // E
    J = HID // P
    CB = C - P
    QC = N // BANK
    TPC = BANK // P
    NT = QC * E * J
    assert (N, C, CB, QC, HC * NH) == (1024, 192, 64, 2, C) and KROWS[0] <= P

    scratch = nc.dram_tensor("padded_scratch", [C, XP], F32, kind="Internal").ap()
    inside_taps = nc.dram_tensor("inside_taps", [len(TAPS), SL], F32, kind="Internal").ap()
    mask_scratch = nc.dram_tensor("inside_scratch", [XP], F32, kind="Internal").ap()

    with ExitStack() as ctx:
        base = (nc.sbuf_base + 31) // 32 * 32
        place = [0]

        def at(name, shape, dt, offset):
            return nc.alloc_sbuf_tensor_at(name, shape, dt, offset=base + offset)

        def size(shape, dt):
            n = 1
            for s in shape[1:]:
                n *= s
            return (n * (2 if dt == BF16 else 4) + 31) // 32 * 32

        def sb(name, shape, dt=F32):
            t = at(name, shape, dt, place[0])
            place[0] += size(shape, dt)
            return t

        def sb_split(name, shape):
            hi = sb(name + "_hi", shape, F32R)
            src = at(name + "_src", shape, F32, place[0])
            lo = sb(name + "_lo", shape, F32R)
            return hi, lo, src

        w1a_hi, w1a_lo, w1a_src = sb_split("w1a", [P, E * HID])
        w1b_hi, w1b_lo, w1b_src = sb_split("w1b", [P, E * HID])
        w2_hi, w2_lo, w2_src = sb_split("w2", [P, E * J, C])
        wqa_hi, wqa_lo, wqa_src = sb_split("wqkv_a", [P, 3 * C])
        wqb_hi, wqb_lo, wqb_src = sb_split("wqkv_b", [P, 3 * C])
        wga_hi, wga_lo, wga_src = sb_split("wgate_a", [P, E])
        wgb_hi, wgb_lo, wgb_src = sb_split("wgate_b", [P, E])
        wconv = [sb(f"wconv{s}", [P, NH, CM]) for s in range(2)]
        wf_t = sb("wf_t", [HALF, 2, C])
        w2pa = sb("wproj2_a", [P, C])
        w2pb = sb("wproj2_b", [CB, C])
        b2p_bc = sb("bproj2_bc", [P, C])
        bf_bc = sb("bf_bc", [P, C])
        gb_bc = sb("gate_b_bc", [P, E])
        b1_sb = sb("b1_sb", [P, E * J])
        convb = sb("convb", [CM, NH])
        ralpha = sb("ralpha", [HALF, 2])
        ident = sb("ident", [P, P])
        ident_r = sb("ident_r", [P, P], F32R)
        ident_bf = sb("ident_bf", [P, P], BF16)
        keep_q = sb("mask_rows_q", [P, P], BF16)
        keep_k = sb("mask_rows_k", [P, P], BF16)
        block_mask = sb("block_mask", [HALF, HALF])
        ones_avg = sb("ones_avg", [HALF, HALF])
        ones32 = sb("ones32", [P, D])
        before = sb("before", [P, E, E])
        minus_half = sb("minus_half", [P, 8])
        pstat = sb("pstat", [HALF, 4, 6])
        pmv = sb("pmv", [HALF, 2])
        img = sb("img", [HALF, 8])
        lm = sb("lm", [HALF, 2, HALF])
        attn_t = sb("attn_t", [HALF, 2, HALF])
        mix = sb("mix", [HALF, 2, C])
        sm = sb("sm", [HALF, 8])
        tstat = sb("tstat", [P, NC, 6])
        tmv = sb("tmv", [P, NC, 2])
        rstd = sb("rstd", [P, 2, NC])
        mx = sb("mx", [P, NC, H])
        mneg = [sb(f"mneg{g}", [P, NC, len(hs), 2], F32R) for g, hs in enumerate(GROUPS)]
        gs = sb("gs", [P, NC, E])
        gx = sb("gx", [P, NC, E])
        gcmp = sb("gcmp", [P, NC, E, E])
        geq = sb("geq", [P, NC, E, E])
        gsum = sb("gsum", [P, NC, 4])
        gate = sb("gate", [P, NC, E])
        t_sb = sb("t_sb", [P, NC, C])
        xn_at = place[0]
        xn = sb("xn", [HALF, 2, N])
        v_sb = at("v_sb", [P, NC, C], F32, xn_at)
        R_T = place[0]
        T0 = sb("T0_hi", [P, N], F32R)
        T1 = sb("T1", [P, N], F32R)
        T2 = sb("T2_lo", [P, N], F32R)
        mrow = [at(f"mrow{g}", [2 * len(hs), N], F32R, R_T + 4096 * g) for g, hs in enumerate(GROUPS)]
        R = place[0]
        K = 1024
        ring = [[at(f"ring{s}_{k}", [P, 2, SL], F32, R + s * 17408 + k * 8704) for k in range(2)] for s in range(2)]
        xhat = at("xhat", [P, NC, 2 * P], F32, R)
        QS = at("QS", [P, H, N], F32R, R)
        KS = at("KS", [P, H, N], F32R, R + 24 * K)
        x_sb = at("x_sb", [HALF, 2, N], F32, R + 34 * K)
        qkve = [at(f"qkve{s}", [CM, N], F32, R + 34 * K + 4 * K * s) for s in range(2)]
        xpad = at("xpad", [HALF, 2, XP], F32, R + 34 * K)
        gb_sb = at("gb_sb", [HALF, 2, N], F32, R + 42 * K)
        qkt = at("qkt", [P, NC, 2, C], F32, R + 42 * K)
        QKh = at("QKh", [P, 3, N], F32R, R + 48 * K)
        QKl = at("QKl", [P, 3, N], F32R, R + 60 * K)
        aTa = at("aTa", [P, N], F32, R + 48 * K)
        aTb = at("aTb", [CB, N], F32, R + 52 * K)
        vp = at("vp", [HALF, 2, N], F32, R + 54 * K)
        PT = at("PT", [P, 8, BANK], F32, R + 56 * K)
        g32 = at("g32", [P, 2, BANK], F32, R + 50 * K)
        g_hi = at("g_hi", [P, 2, BANK], F32R, R + 54 * K)
        g_lo = at("g_lo", [P, 2, BANK], F32R, R + 58 * K)
        b2_bc = at("b2_bc", [P, E, C], F32, R + 62 * K)
        outs_a = at("outs_a", [P, QC, BANK], F32, R + 65 * K)
        outs_b = at("outs_b", [CB, QC, BANK], F32, R + 69 * K)
        rc = at("rc", [P, BANK], F32, R + 73 * K)
        wp_src = [at(f"wp_src{i}", [P, C], F32, R + 65 * K + 768 * i) for i in range(4)]
        bp_src = at("bp_src", [P, 2], F32, R + 69 * K)
        bp_row = at("bp_row", [P, 2, P], F32, R + 70 * K)
        bpb = at("bpb", [P, C], F32, R + 72 * K)
        wtap = [at(f"wtap{s}", [P, NH, CM], F32, R + 54 * K + 3 * K * s) for s in range(2)]
        inside = at("inside", [1, XP], F32, R + 60 * K)
        ctx.enter_context(nc.sbuf_tensor("whole_map", [P, (R + 75 * K) // 4], F32))
        ps = ctx.enter_context(nc.psum_tensor("ps", [P, 8 * BANK], F32))

        def bank(b, n=1):
            return ps[:, b * BANK:(b + n) * BANK]

        names = []

        def sem(name):
            s = ctx.enter_context(nc.semaphore(name))
            names.append(s)
            return s

        conv_ps, qkT_ps, logit_ps, attnT_ps, mix_ps, y_ps = map(sem, "conv_ps qkT_ps logit_ps attnT_ps mix_ps y_ps".split())
        lnT_ps, qk_ps, v_ps, s_ps, mT_ps, st_ps, p_used, o_ps = map(
            sem, "lnT_ps qk_ps v_ps s_ps mT_ps st_ps p_used o_ps".split())
        gate_ps, up_ps, down_ps, stat_ps, outT_ps = map(sem, "gate_ps up_ps down_ps stat_ps outT_ps".split())
        conv_sb, e_sb, mix_sb, T_hi, qk_hi, v_done, mrow_sb, p_sb, gexp_sb, gelu_sb, out_sb = map(
            sem, "conv_sb e_sb mix_sb T_hi qk_hi v_done mrow_sb p_sb gexp_sb gelu_sb out_sb".split())
        chain, qkT_sb, lm_sb, attn_sb, attnT_sb, y_sb, veps, xhat_sb, T_lo, qk_lo, mx_sb, mneg_sb, at_sb, o_sb = map(
            sem, "chain qkT_sb lm_sb attn_sb attnT_sb y_sb veps xhat_sb T_lo qk_lo mx_sb mneg_sb at_sb o_sb".split())
        gsub, lo_sb, t_acc, acc_sb, xstat, img_veps, xg_sb, xn_sb = map(
            sem, "gsub lo_sb t_acc acc_sb xstat img_veps xg_sb xn_sb".split())
        rstd_sb, tb_sb, ks_ones, img_rstd, pad_zero, padded = map(sem, "rstd_sb tb_sb ks_ones img_rstd pad_zero padded".split())
        ring_ld = [sem(f"ring_ld{p}") for p in range(4)]
        v_dma = [sem(f"v_dma{p}") for p in range(2)]
        stack_ld = [sem(f"stack_ld{h}") for h in range(H)]
        m_ld = [sem(f"m_ld{g}") for g in range(2)]
        b2_ld, x_ld, g_ld, b_ld, scr_w = map(sem, "b2_ld x_ld g_ld b_ld scr_w".split())
        started = sem("started")
        per_image = range(names[0].num, names[-1].num + 1)
        assert [s.num for s in names] == list(per_image)
        next_image, dram_written = map(sem, "next_image dram_written".split())
        w_ld = {k: sem("w_ld_" + k) for k in "conv small proj gate qkv w1a w1b w2 inside".split()}
        setup_pool, inside_zero, setup_dve, setup_pe, setup_ready = map(
            sem, "setup_pool inside_zero setup_dve setup_pe setup_ready".split())
        RING = 16 * (len(TAPS) + len(STACKS))

        block = ctx.enter_context(nc.Block())

        def load_ring(sp, p):
            for s, taps in enumerate(STACKS):
                dst = ring[p % 2][s]
                for j, tap in enumerate(taps):
                    src = scratch[2 * p * HC:2 * (p + 1) * HC, SHIFT[tap]:SHIFT[tap] + SL]
                    sp.dma_start(dst[HC * j:HC * (j + 1), :, :],
                                 src.rearrange("(h c) l -> c h l", c=HC)).then_inc(ring_ld[p], 16)
                nt = len(taps)
                sp.dma_start(dst[HC * nt:HC * nt + nt, :, :],
                             inside_taps[taps[0]:taps[0] + nt, :].unsqueeze(1).to_broadcast([nt, 2, SL])
                             ).then_inc(ring_ld[p], 16)

        def load_image(sp, i):
            sp.dma_start(x_sb[:, :, :], x[i].rearrange("(h p) a b -> p h (a b)", h=2)).then_inc(x_ld, 16)
            sp.dma_start(gb_sb[:, :, :], ln_g.rearrange("(h p) a b -> p h (a b)", h=2)).then_inc(g_ld, 16)

        def load_shift(sp):
            sp.wait_ge(xg_sb, 2)
            sp.dma_start(gb_sb[:, :, :], ln_b.rearrange("(h p) a b -> p h (a b)", h=2)).then_inc(b_ld, 16)

        def store_padded(sp):
            sp.wait_ge(padded, 2)
            sp.dma_start(scratch.rearrange("(h p) l -> p h l", h=2), xpad[:, :, :]).then_inc(scr_w, 16)
            sp.wait_ge(scr_w, 16)

        def chained(dve):
            count = [0]

            def link(ins):
                count[0] += 1
                ins.then_inc(chain, 1)
                dve.wait_ge(chain, count[0])
            return link

        def image_norm_steps(dve, link):
            v = nc.vector

            def stats(q):
                if q == 0:
                    dve.wait_ge(x_ld, 16)
                ins = v.bn_stats(pstat[:, q, :], x_sb[:, q // 2, BANK * (q % 2):BANK * (q % 2 + 1)])
                if q == 3:
                    link(ins)

            def partition_mean():
                v.bn_aggr(pmv[:, :], pstat[:, :, :]).then_inc(xstat, 1)

            def deviation():
                dve.wait_ge(xstat, 1)
                dve.wait_ge(stat_ps, 1)
                link(v.tensor_copy(img[:, 0:1], bank(2)[0:HALF, 0:1]))
                link(v.tensor_tensor(img[:, 1:2], pmv[:, 0:1], img[:, 0:1], ALU.subtract))
                link(v.tensor_tensor(img[:, 2:3], img[:, 1:2], img[:, 1:2], ALU.mult))
                v.tensor_tensor(img[:, 3:4], img[:, 2:3], pmv[:, 1:2], ALU.add).then_inc(xstat, 1)

            def variance():
                dve.wait_ge(stat_ps, 2)
                v.tensor_scalar(img[:, 4:5], bank(2)[0:HALF, 1:2], 1e-5, None, ALU.add).then_inc(img_veps, 1)

            def gain(h):
                if h == 0:
                    dve.wait_ge(g_ld, 16)
                v.scalar_tensor_tensor(out=x_sb[:, h, :], in0=x_sb[:, h, :], scalar=img[:, 0:1],
                                       in1=gb_sb[:, h, :], op0=ALU.subtract, op1=ALU.mult).then_inc(xg_sb, 1)

            def shift(h):
                if h == 0:
                    dve.wait_ge(b_ld, 16)
                    dve.wait_ge(img_rstd, 1)
                    dve.wait_ge(xg_sb, 2)
                v.scalar_tensor_tensor(out=xn[:, h, :], in0=x_sb[:, h, :], scalar=img[:, 5:6], in1=gb_sb[:, h, :],
                                       op0=ALU.mult, op1=ALU.add).then_inc(xn_sb, 1)

            return stats, partition_mean, deviation, variance, gain, shift

        def start_image(eng, i):
            eng.wait_ge(next_image, i + 1)
            eng.sem_inc(started, 1)

        def average_mean(pe):
            pe.wait_ge(xstat, 1)
            nc.tensor.matmul(bank(2)[0:HALF, 0:1], ones_avg[:, :], pmv[:, 0:1], start=True, stop=True).then_inc(stat_ps, 1)

        def average_var(pe):
            pe.wait_ge(xstat, 2)
            nc.tensor.matmul(bank(2)[0:HALF, 1:2], ones_avg[:, :], img[:, 3:4], start=True, stop=True).then_inc(stat_ps, 1)

        def image_rstd(pool):
            pool.wait_ge(img_veps, 1)
            nc.gpsimd.tensor_tensor(img[:, 5:6], img[:, 4:5], minus_half[0:HALF, 0:1], ALU.pow).then_inc(img_rstd, 1)

        def pad_image(pool):
            pool.wait_ge(xn_sb, 2)
            nc.gpsimd.memset(xpad[:, :, :], 0.0).then_inc(pad_zero, 1)
            pool.wait_ge(pad_zero, 1)
            for h in range(2):
                inner = xpad[:, h, 0:PW * (SH + 2)].rearrange("p (a b) -> p a b", b=PW)[:, 1:SH + 1, 1:SW + 1]
                nc.gpsimd.tensor_copy(inner, xn[:, h, :].rearrange("p (a b) -> p a b", b=SW)).then_inc(padded, 1)

        STEPS = [(g, c, kb) for g in range(2) for c in range(QC) for kb in range(TPC * (c + 1))]
        first_tile = []
        n = 0
        for g, c, kb in STEPS:
            first_tile.append(n)
            n += len(GROUPS[g])
        step_of_tile = [s for s, (g, _, _) in enumerate(STEPS) for _ in GROUPS[g]]

        def half_done(g, c):
            return max(s for s, (gg, cc, _) in enumerate(STEPS) if (gg, cc) == (g, c)) + 1

        def query_range(c, kb):
            off = P * (kb - TPC * c) if kb >= TPC * c else 0
            return off, BANK - off

        M0_SLOT = NC * (H - 1)
        OUT0 = 30

        def added(idx):
            return min(J * (idx + 1) + 1, NC * E) + TPC * (idx + 1)

        @block.sync
        def _(sp):
            load_image(sp, 0)
            sp.dma_start(wp_src[0][0:P, :], w_proj[0:P, :]).then_inc(w_ld["proj"], 16)
            sp.dma_start(wp_src[1][0:CB, :], w_proj[P:C, :]).then_inc(w_ld["proj"], 16)
            sp.dma_start(wp_src[2][0:P, :], w_proj_t[0:P, :]).then_inc(w_ld["proj"], 16)
            sp.dma_start(wp_src[3][0:CB, :], w_proj_t[P:C, :]).then_inc(w_ld["proj"], 16)
            sp.dma_start(bp_src[:, 0:1], b_proj[0:P].rearrange("(p a) -> p a", a=1)).then_inc(w_ld["proj"], 16)
            sp.dma_start(bp_src[0:CB, 1:2], b_proj[P:C].rearrange("(p a) -> p a", a=1)).then_inc(w_ld["proj"], 16)
            sp.dma_start(bpb[:, :], b_proj.partition_broadcast(P)).then_inc(w_ld["proj"], 16)
            sp.dma_start(bf_bc[:, :], b_f.partition_broadcast(P)).then_inc(w_ld["small"], 16)
            sp.dma_start(gb_bc[:, :], gate_b.partition_broadcast(P)).then_inc(w_ld["small"], 16)
            sp.dma_start(b1_sb[:, :], b1_t).then_inc(w_ld["small"], 16)
            sp.dma_start(convb[:, :], conv_bias).then_inc(w_ld["small"], 16)
            sp.dma_start(wf_t[:, :, :], w_f_t.rearrange("(h p) o -> p h o", h=2)).then_inc(w_ld["small"], 16)
            sp.dma_start(ralpha[:, :], alpha_rows).then_inc(w_ld["small"], 16)
            sp.wait_ge(setup_pool, 2)
            sp.dma_start(mask_scratch.rearrange("(a l) -> a l", a=1), inside[:, :]).then_inc(w_ld["inside"], 16)
            sp.wait_ge(w_ld["inside"], 16)
            for tap in TAPS:
                sp.dma_start(inside_taps[tap:tap + 1, :],
                             mask_scratch[SHIFT[tap]:SHIFT[tap] + SL].rearrange("(a l) -> a l", a=1)
                             ).then_inc(dram_written, 16)
            sp.wait_ge(setup_pool, 1)
            for s, taps in enumerate(STACKS):
                nt = len(taps)
                for j, tap in enumerate(taps):
                    sp.dma_start(wconv[s][HC * j:HC * (j + 1), :, :], conv_w).then_inc(w_ld["conv"], 16)
                    sp.dma_start(wtap[s][HC * j:HC * (j + 1), :, :],
                                 conv_taps[tap].partition_broadcast(HC)).then_inc(w_ld["conv"], 16)
                sp.dma_start(wconv[s][HC * nt:HC * nt + nt, :, :],
                             conv_bias_row.partition_broadcast(nt)).then_inc(w_ld["conv"], 16)
                sp.dma_start(wtap[s][HC * nt:HC * nt + nt, :, :],
                             conv_taps[taps[0]:taps[0] + nt]).then_inc(w_ld["conv"], 16)
            sp.dma_start(wga_src[:, :], gate_w_a).then_inc(w_ld["gate"], 16)
            sp.dma_start(wgb_src[:, :], gate_w_b).then_inc(w_ld["gate"], 16)
            sp.dma_start(wqa_src[:, :], w_qkv_a).then_inc(w_ld["qkv"], 16)
            sp.dma_start(wqb_src[:, :], w_qkv_b).then_inc(w_ld["qkv"], 16)
            load_shift(sp)
            sp.dma_start(w1a_src[:, :], w1_a).then_inc(w_ld["w1a"], 16)
            sp.dma_start(w1b_src[:, :], w1_b).then_inc(w_ld["w1b"], 16)
            sp.dma_start(w2_src[:, :, :], w2).then_inc(w_ld["w2"], 16)
            store_padded(sp)
            sp.wait_ge(dram_written, 16 * len(TAPS))
            for p in range(2):
                load_ring(sp, p)
            for p in range(2):
                sp.wait_ge(ring_ld[p], RING)
            for s in (x_ld, g_ld, b_ld):
                sp.wait_ge(s, 16)
            sp.wait_ge(setup_ready, 4)
            sp.sem_clear(per_image)
            sp.sem_inc(next_image, 1)

            with sp.Fori(0, B) as i:
                for h in range(NH):
                    if h in (2, 4):
                        p = 2 + (h - 2) // 2
                        sp.wait_ge(conv_ps, h)
                        load_ring(sp, p)
                    sp.wait_ge(conv_sb, h + 1)
                    if h == NH - 1:
                        sp.wait_ge(dram_written, i * (32 * QC) + 16 * len(TAPS))
                    sp.dma_start(vp[HC * (h % HPH):HC * (h % HPH + 1), h // HPH, :],
                                 qkve[h % 2][64:64 + HC, :]).then_inc(v_dma[h % 2], 16)
                for h in range(H):
                    if h == 0:
                        sp.wait_ge(qk_lo, 5)
                    if h == 4:
                        sp.wait_ge(qk_lo, 6)
                    fq, fk = (0, 1) if h < 4 else (2, 2)
                    rq = D * h if h < 4 else D * (h - 4)
                    rk = D * h if h < 4 else 64 + D * (h - 4)
                    for r, (part) in enumerate((QKh, QKl, QKh)):
                        sp.dma_start(QS[D * r:D * (r + 1), h, :].bitcast(F32), part[rq:rq + D, fq, :].bitcast(F32)).then_inc(stack_ld[h], 16)
                    for r, (part) in enumerate((QKh, QKh, QKl)):
                        sp.dma_start(KS[D * r:D * (r + 1), h, :].bitcast(F32), part[rk:rk + D, fk, :].bitcast(F32)).then_inc(stack_ld[h], 16)
                for g, hs in enumerate(GROUPS):
                    sp.wait_ge(mrow_sb, g + 1)
                    for j, h in enumerate(hs):
                        sp.dma_start(QS[96:98, h, :].bitcast(F32), mrow[g][2 * j:2 * j + 2, :].bitcast(F32)).then_inc(m_ld[g], 16)
                sp.wait_ge(o_ps, NC)
                load_image(sp, (i + 1) % B)
                sp.dma_start(b2_bc[:, :, :], b2.partition_broadcast(P)).then_inc(b2_ld, 16)
                load_shift(sp)
                store_padded(sp)
                sp.wait_ge(lnT_ps, 8)
                for p in range(2):
                    sp.wait_ge(ring_ld[p + 2], RING)
                    load_ring(sp, p)
                for c in range(QC):
                    sp.wait_ge(out_sb, 2 * c + 2)
                    o_img = out[i].rearrange("c a b -> c (a b)")
                    sp.dma_start(o_img[0:P, BANK * c:BANK * (c + 1)], outs_a[:, c, :]).then_inc(dram_written, 16)
                    sp.dma_start(o_img[P:C, BANK * c:BANK * (c + 1)], outs_b[:, c, :]).then_inc(dram_written, 16)
                for p in range(2):
                    sp.wait_ge(ring_ld[p], RING)
                for s in (x_ld, g_ld, b_ld, b2_ld):
                    sp.wait_ge(s, 16)
                sp.sem_clear(per_image)
                sp.sem_inc(next_image, 1)
            sp.wait_ge(dram_written, B * 32 * QC + 16 * len(TAPS))

        @block.gpsimd
        def _(pool):
            g = nc.gpsimd
            g.memset(wconv[0][:, :, :], 0.0)
            g.memset(wconv[1][:, :, :], 0.0)
            g.memset(wtap[0][:, :, :], 0.0)
            g.memset(wtap[1][:, :, :], 0.0).then_inc(setup_pool, 1)
            g.memset(inside[:, :], 0.0).then_inc(inside_zero, 1)
            pool.wait_ge(inside_zero, 1)
            g.memset(inside[:, 0:PW * (SH + 2)].rearrange("p (a b) -> p a b", b=PW)[:, 1:SH + 1, 1:SW + 1], 1.0
                     ).then_inc(setup_pool, 1)
            g.memset(minus_half[:, :], -0.5)
            g.memset(ones_avg[:, :], 1.0 / HALF)
            g.memset(ones32[:, :], 1.0)
            g.memset(before[:, :, :], 0.0)
            g.memset(block_mask[:, :], 0.0)
            g.memset(ident[:, :], 0.0)
            g.memset(ident_bf[:, :], 0.0)
            g.memset(keep_q[:, :], 0.0)
            g.memset(keep_k[:, :], 0.0).then_inc(setup_pool, 1)
            pool.wait_ge(setup_pool, 3)
            for m in (ident, ident_bf):
                g.affine_select(out=m[:, :], in_=m[:, :], compare_op=ALU.not_equal, fill=1.0, base=0,
                                pattern=[[-1, P]], channel_multiplier=1)
            g.affine_select(out=keep_q[:, :], in_=keep_q[:, :], compare_op=ALU.is_ge, fill=NEG, base=0,
                            pattern=[[-1, P]], channel_multiplier=1)
            g.affine_select(out=keep_k[:, :], in_=keep_k[:, :], compare_op=ALU.is_ge, fill=NEG, base=0,
                            pattern=[[1, P]], channel_multiplier=-1)
            g.affine_select(out=before[:, :, :], in_=before[:, :, :], compare_op=ALU.is_ge, fill=1.0, base=0,
                            pattern=[[-1, E], [1, E]], channel_multiplier=0)
            bm = block_mask[:, :].rearrange("p (h c) -> p h c", c=HC)
            g.affine_select(out=bm, in_=bm, compare_op=ALU.is_ge, fill=NEG, base=0,
                            pattern=[[-HC, HPH], [0, HC]], channel_multiplier=1).then_inc(setup_pool, 1)
            pool.wait_ge(setup_pool, 4)
            g.affine_select(out=bm, in_=bm, compare_op=ALU.is_ge, fill=NEG, base=HC - 1,
                            pattern=[[HC, HPH], [0, HC]], channel_multiplier=-1).then_inc(setup_pool, 1)
            image_rstd(pool)
            pad_image(pool)
            pool.wait_ge(padded, 2)
            pool.sem_inc(setup_ready, 1)

            with pool.Fori(0, B) as i:
                start_image(pool, i)
                pool.wait_ge(veps, 1)
                g.tensor_tensor(rstd[:, 1, :], rstd[:, 0, :], minus_half[:, 0:NC], ALU.pow).then_inc(rstd_sb, 1)
                pool.wait_ge(xhat_sb, NC)
                g.tensor_tensor(t_sb[:, :, :], t_sb[:, :, :],
                                b2p_bc[:, :].unsqueeze(1).to_broadcast([P, NC, C]), ALU.add).then_inc(tb_sb, 1)
                pool.wait_ge(tb_sb, 1)
                g.memset(KS[96:98, :, :].bitcast(F32), 1.0).then_inc(ks_ones, 1)
                pool.wait_ge(veps, 2)
                g.tensor_tensor(rstd[:, 1, :], rstd[:, 0, :], minus_half[:, 0:NC], ALU.pow).then_inc(rstd_sb, 1)
                image_rstd(pool)
                pad_image(pool)

        @block.vector
        def _(dve):
            v = nc.vector
            link = chained(dve)
            stats, partition_mean, deviation, variance, gain, shift = image_norm_steps(dve, link)
            for q in range(4):
                stats(q)
            partition_mean()
            dve.wait_ge(setup_pool, 5)
            v.tensor_copy(ident_r[:, :], ident[:, :]).then_inc(setup_dve, 1)
            deviation()
            dve.wait_ge(w_ld["proj"], 16 * 7)
            for k, rows in enumerate((P, CB)):
                v.tensor_copy(bp_row[0:rows, k, :], bp_src[0:rows, k:k + 1].to_broadcast([rows, P])
                              ).then_inc(setup_dve, 1)
            variance()
            for h in range(2):
                gain(h)
            dve.wait_ge(w_ld["small"], 16 * 6)
            link(v.reciprocal(ralpha[:, :], ralpha[:, :]))
            dve.wait_ge(setup_pe, 1)
            v.tensor_copy(w2pa[:, :], bank(0)[:, 0:C])
            v.tensor_copy(w2pb[:, :], bank(1)[0:CB, 0:C])
            link(v.tensor_tensor(b2p_bc[:, :], bank(3)[:, 0:C], bpb[:, :], ALU.add))
            dve.wait_ge(w_ld["conv"], 16 * (2 * len(TAPS) + 4))
            for s in range(2):
                link(v.tensor_tensor(wconv[s][:, :, :], wconv[s][:, :, :], wtap[s][:, :, :], ALU.mult))
            for h in range(2):
                shift(h)
            for key, sets in (("gate", ((wga_hi, wga_lo, wga_src), (wgb_hi, wgb_lo, wgb_src))),
                              ("qkv", ((wqa_hi, wqa_lo, wqa_src), (wqb_hi, wqb_lo, wqb_src))),
                              ("w1a", ((w1a_hi, w1a_lo, w1a_src),)), ("w1b", ((w1b_hi, w1b_lo, w1b_src),)),
                              ("w2", ((w2_hi, w2_lo, w2_src),))):
                dve.wait_ge(w_ld[key], 16 * len(sets))
                for hi, lo, src in sets:
                    full = tuple(slice(None) for _ in src.shape)
                    link(v.tensor_copy(hi[full], src[full]))
                    link(v.tensor_tensor(lo[full], src[full], hi[full].bitcast(F32), ALU.subtract))
            dve.wait_ge(xn_sb, 2)
            dve.wait_ge(setup_dve, 3)
            dve.sem_inc(setup_ready, 1)

            with dve.Fori(0, B) as i:
                start_image(dve, i)
                link = chained(dve)
                stats, partition_mean, deviation, variance, gain, shift = image_norm_steps(dve, link)
                for h in range(NH):
                    dve.wait_ge(qkT_ps, h + 1)
                    src = bank(4 + h % 2).rearrange("p (k j c) -> p k j c", j=2, c=32)[:, :, :, 0:HC]
                    v.tensor_copy(qkt[:, :, :, HC * h:HC * (h + 1)], src).then_inc(qkT_sb, 1)
                for f in range(2):
                    dve.wait_ge(logit_ps, f + 1)
                    link(v.scalar_tensor_tensor(out=lm[:, f, :], in0=bank(6 + f)[0:HALF, 0:HALF],
                                                scalar=ralpha[:, f:f + 1], in1=block_mask[:, :],
                                                op0=ALU.mult, op1=ALU.add))
                    v.tensor_reduce(sm[:, f:f + 1], lm[:, f, :], AX, ALU.max, negate=True).then_inc(lm_sb, 1)
                for f in range(2):
                    dve.wait_ge(e_sb, f + 1)
                    link(v.reciprocal(sm[:, 4 + f:5 + f], sm[:, 2 + f:3 + f]))
                    v.tensor_scalar(lm[:, f, :], lm[:, f, :], sm[:, 4 + f:5 + f], None, ALU.mult).then_inc(attn_sb, 1)
                for f in range(2):
                    dve.wait_ge(attnT_ps, f + 1)
                    v.tensor_copy(attn_t[:, f, :], bank(6 + f)[0:HALF, P:P + HALF]).then_inc(attnT_sb, 1)

                def token_norm(a):
                    v.tensor_scalar(rstd[:, 0, :], tmv[:, :, 1], 1e-5, None, ALU.add).then_inc(veps, 1)
                    dve.wait_ge(rstd_sb, a + 1)
                    for k in range(NC):
                        v.tensor_scalar(xhat[:, k, 0:C], t_sb[:, k, :], tmv[:, k, 0:1], rstd[:, 1, k:k + 1],
                                        ALU.subtract, ALU.mult)
                        v.tensor_scalar(xhat[:, k, C:2 * P], t_sb[:, k, P:C], tmv[:, k, 0:1], rstd[:, 1, k:k + 1],
                                        ALU.subtract, ALU.mult).then_inc(xhat_sb, 1)
                    for j in range(QC):
                        cols = slice(BANK * j, BANK * (j + 1))
                        dve.wait_ge(T_hi, 4 * a + 2 * j + 1)
                        v.tensor_tensor(T2[:, cols], bank(j), T0[:, cols].bitcast(F32), ALU.subtract).then_inc(T_lo, 1)
                        dve.wait_ge(T_hi, 4 * a + 2 * j + 2)
                        v.tensor_tensor(T1[64:P, cols], bank(2 + j)[64:P, :], T1[64:P, cols].bitcast(F32),
                                        ALU.subtract).then_inc(T_lo, 1)

                def token_stats(k, done, count):
                    dve.wait_ge(done, count)
                    link(v.bn_stats(tstat[:, k, :], t_sb[:, k, :]))
                    link(v.bn_aggr(tmv[:, k, :], tstat[:, k, :]))

                for k in range(NC):
                    dve.wait_ge(y_ps, k + 1)
                    v.tensor_tensor(t_sb[:, k, :], bank(k % 4)[:, 0:C], bf_bc[:, :], ALU.add).then_inc(y_sb, 1)
                    if k:
                        token_stats(k - 1, y_sb, k)
                token_stats(NC - 1, y_sb, NC)
                token_norm(0)
                for n in range(6):
                    f, nh = n % 3, n // 3
                    dve.wait_ge(qk_hi, n + 1)
                    v.tensor_tensor(QKl[:, f, BANK * nh:BANK * (nh + 1)], bank(4 + n % 4),
                                    QKh[:, f, BANK * nh:BANK * (nh + 1)].bitcast(F32), ALU.subtract).then_inc(qk_lo, 1)
                for h in range(H):
                    for qc in range(NC):
                        n = NC * h + qc
                        r = n if n < M0_SLOT else n + 1
                        dve.wait_ge(s_ps, n + 1)
                        v.tensor_reduce(mx[:, qc, h:h + 1], bank(2 * (r % 4), 2)[:, 0:P * (qc + 1)], AX, ALU.max
                                        ).then_inc(mx_sb, 1)
                    for g, hs in enumerate(GROUPS):
                        if h == hs[-1]:
                            dve.wait_ge(mx_sb, NC * (h + 1))
                            src = mx[:, :, hs[0]:hs[-1] + 1]
                            link(v.tensor_scalar(mneg[g][:, :, :, 0], src, -1.0, None, ALU.mult))
                            v.scalar_tensor_tensor(out=mneg[g][:, :, :, 1], in0=src, scalar=-1.0,
                                                   in1=mneg[g][:, :, :, 0].bitcast(F32),
                                                   op0=ALU.mult, op1=ALU.subtract).then_inc(mneg_sb, 1)
                for g, hs in enumerate(GROUPS):
                    rows = D * len(hs)
                    dst = (aTa, aTb)[g]
                    for c in range(QC):
                        dve.wait_ge(p_used, half_done(g, c))
                        sums = bank(2 * c + 1)[0:rows, :] if g == 0 else bank(2 * c)[64:P, :]
                        link(v.reciprocal(rc[0:rows, :], sums))
                        v.tensor_tensor(dst[0:rows, BANK * c:BANK * (c + 1)], bank(2 * c)[0:rows, :], rc[0:rows, :],
                                        ALU.mult).then_inc(at_sb, 1)
                        dve.wait_ge(at_sb, QC * g + c + 1)
                dve.wait_ge(tb_sb, 1)
                for k in range(NC):
                    dve.wait_ge(o_ps, k + 1)
                    v.tensor_tensor(t_sb[:, k, :], bank(4 + k % 4)[:, 0:C], t_sb[:, k, :], ALU.add).then_inc(o_sb, 1)
                    if k:
                        token_stats(k - 1, o_sb, k)
                token_stats(NC - 1, o_sb, NC)
                token_norm(1)

                count = [0]
                last = [0] * NC

                def onto_tokens(k, ins):
                    if last[k]:
                        dve.wait_ge(t_acc, last[k])
                    count[0] += 1
                    last[k] = count[0]
                    return ins().then_inc(t_acc, 1)

                def gating():
                    bc = lambda a: a.unsqueeze(2).to_broadcast([P, NC, E])
                    dve.wait_ge(gate_ps, 1)
                    src = bank(7)[:, 0:NC * E].rearrange("p (k e) -> p k e", e=E)
                    link(v.tensor_tensor(gs[:, :, :], src, gb_bc[:, :].unsqueeze(1).to_broadcast([P, NC, E]), ALU.add))
                    link(v.tensor_reduce(gsum[:, :, 0], gs[:, :, :], AX, ALU.max))
                    v.tensor_tensor(gs[:, :, :], gs[:, :, :], bc(gsum[:, :, 0]), ALU.subtract).then_inc(gsub, 1)

                def routing():
                    bc = lambda a: a.unsqueeze(2).to_broadcast([P, NC, E])
                    dve.wait_ge(gexp_sb, 1)
                    other = gx[:, :, :].unsqueeze(2).to_broadcast([P, NC, E, E])
                    mine = gx[:, :, :].unsqueeze(3).to_broadcast([P, NC, E, E])
                    for e in range(E):
                        o, m = other[:, :, e, :], mine[:, :, e, :]
                        v.tensor_tensor(gcmp[:, :, e, :], o, m, ALU.is_gt)
                        last_eq = v.tensor_tensor(geq[:, :, e, :], o, m, ALU.is_equal)
                    link(last_eq)
                    for e in range(E):
                        last_eq = v.tensor_tensor(geq[:, :, e, :], geq[:, :, e, :],
                                                  before[:, e, :].unsqueeze(1).to_broadcast([P, NC, E]), ALU.mult)
                    link(last_eq)
                    link(v.tensor_tensor(gcmp[:, :, :, :], gcmp[:, :, :, :], geq[:, :, :, :], ALU.add))
                    link(v.tensor_reduce(gs[:, :, :], gcmp[:, :, :, :], AX, ALU.add))
                    link(v.scalar_tensor_tensor(out=gate[:, :, :], in0=gs[:, :, :], scalar=1.5, in1=gx[:, :, :],
                                                op0=ALU.is_lt, op1=ALU.mult))
                    v.tensor_reduce(gsum[:, :, 1], gate[:, :, :], AX, ALU.add)
                    link(v.tensor_reduce(gsum[:, :, 2], gx[:, :, :], AX, ALU.add))
                    link(v.scalar_tensor_tensor(out=gsum[:, :, 3], in0=gsum[:, :, 2], scalar=1e-9, in1=gsum[:, :, 1],
                                                op0=ALU.mult, op1=ALU.add))
                    link(v.reciprocal(gsum[:, :, 1], gsum[:, :, 3]))
                    link(v.tensor_tensor(gate[:, :, :], gate[:, :, :], bc(gsum[:, :, 1]), ALU.mult))

                def low_part(n):
                    dve.wait_ge(gelu_sb, n + 1)
                    v.tensor_tensor(g_lo[:, n % 2, :], g32[:, n % 2, :], g_hi[:, n % 2, :].bitcast(F32),
                                    ALU.subtract).then_inc(lo_sb, 1)

                def bias_term(m):
                    k, e = m // E, m % E
                    if m == 0:
                        dve.wait_ge(b2_ld, 16)
                    onto_tokens(k, lambda: v.scalar_tensor_tensor(
                        out=t_sb[:, k, :], in0=b2_bc[:, e, :], scalar=gate[:, k, e:e + 1], in1=t_sb[:, k, :],
                        op0=ALU.mult, op1=ALU.add))

                def expert_sum(idx):
                    c, e = idx // E, idx % E
                    dve.wait_ge(down_ps, J * (idx + 1))
                    for tt in range(TPC):
                        k = TPC * c + tt
                        src = bank(4 + 2 * (idx % 2) + tt // 2)[:, C * (tt % 2):C * (tt % 2 + 1)]
                        onto_tokens(k, lambda: v.scalar_tensor_tensor(
                            out=t_sb[:, k, :], in0=src, scalar=gate[:, k, e:e + 1], in1=t_sb[:, k, :],
                            op0=ALU.mult, op1=ALU.add))

                gating()
                image_steps = {4: lambda: stats(0), 5: lambda: stats(1), 6: lambda: stats(2), 7: lambda: stats(3),
                               8: partition_mean, 10: deviation, 12: variance, 14: lambda: gain(0),
                               15: lambda: gain(1), 20: lambda: shift(0), 21: lambda: shift(1)}
                for n in range(NT):
                    low_part(n)
                    if n == 0:
                        routing()
                    if n < NC * E:
                        bias_term(n)
                    if n >= J and n % J == 0:
                        expert_sum(n // J - 1)
                    if n in image_steps:
                        image_steps[n]()
                expert_sum(QC * E - 1)

        @block.scalar
        def _(act):
            a = nc.scalar
            act.sem_inc(setup_ready, 1)

            with act.Fori(0, B) as i:
                start_image(act, i)
                for h in range(NH):
                    act.wait_ge(conv_ps, h + 1)
                    if h >= 2:
                        act.wait_ge(qkT_ps, h - 1)
                        act.wait_ge(v_dma[h % 2], 16 * (h // 2))
                    a.activation(qkve[h % 2][:, :], bank(2 * (h % 2), 2)[0:CM, :], ACT.Identity,
                                 bias=convb[:, h:h + 1]).then_inc(conv_sb, 1)
                for f in range(2):
                    act.wait_ge(lm_sb, f + 1)
                    a.activation(lm[:, f, :], lm[:, f, :], ACT.Exp, bias=sm[:, f:f + 1],
                                 accum_out=sm[:, 2 + f:3 + f]).then_inc(e_sb, 1)
                for f in range(2):
                    act.wait_ge(mix_ps, f + 1)
                    a.activation(mix[:, f, :], bank(6 + f)[0:HALF, 2 * P:2 * P + C], ACT.Copy).then_inc(mix_sb, 1)

                def high_parts(norm):
                    for j in range(QC):
                        for b, dst in ((j, T0), (2 + j, T1)):
                            act.wait_ge(lnT_ps, 4 * norm + 2 * j + (1 if b == j else 2))
                            a.activation(dst[:, BANK * j:BANK * (j + 1)], bank(b), ACT.Copy).then_inc(T_hi, 1)

                high_parts(0)
                for n in range(6):
                    f, nh = n % 3, n // 3
                    act.wait_ge(qk_ps, n + 1)
                    a.activation(QKh[:, f, BANK * nh:BANK * (nh + 1)], bank(4 + n % 4), ACT.Copy).then_inc(qk_hi, 1)
                for k in range(NC):
                    act.wait_ge(v_ps, k + 1)
                    a.activation(v_sb[:, k, :], bank(k % 4)[:, 0:C], ACT.Copy).then_inc(v_done, 1)
                for g, hs in enumerate(GROUPS):
                    act.wait_ge(mT_ps, g + 1)
                    b = 2 * ((M0_SLOT if g == 0 else 1) % 4)
                    a.activation(mrow[g][:, :], bank(b, 2)[0:2 * len(hs), :], ACT.Copy).then_inc(mrow_sb, 1)
                for q, s in enumerate(step_of_tile):
                    g, c, kb = STEPS[s]
                    off, w = query_range(c, kb)
                    act.wait_ge(st_ps, q + 1)
                    if q >= 8:
                        act.wait_ge(p_used, step_of_tile[q - 8] + 1)
                    a.activation(PT[:, q % 8, 0:w], bank(4 + q % 4)[:, 0:w], ACT.Exp, scale=SCALE).then_inc(p_sb, 1)
                high_parts(1)
                act.wait_ge(gsub, 1)
                a.activation(gx[:, :, :], gs[:, :, :], ACT.Exp).then_inc(gexp_sb, 1)

                def outputs(c):
                    for b, dst in ((2, outs_a[:, c, :]), (3, outs_b[:, c, :])):
                        act.wait_ge(outT_ps, 2 * c + b - 1)
                        a.activation(dst, bank(b)[0:P if b == 2 else CB, :], ACT.Copy).then_inc(out_sb, 1)

                for n in range(NT):
                    e, j = n // J % E, n % J
                    act.wait_ge(up_ps, n + 1)
                    if n >= 2:
                        act.wait_ge(down_ps, n - 1)
                        act.wait_ge(lo_sb, n - 1)
                    b1 = b1_sb[:, e * J + j:e * J + j + 1]
                    a.activation(g32[:, n % 2, :], bank(n % 2), ACT.Gelu, bias=b1)
                    a.activation(g_hi[:, n % 2, :], bank(n % 2), ACT.Gelu, bias=b1).then_inc(gelu_sb, 1)
                    if n == OUT0:
                        outputs(0)
                outputs(1)

        @block.tensor
        def _(pe):
            t = nc.tensor

            pe.wait_ge(setup_pool, 5)
            average_mean(pe)
            average_var(pe)
            pe.wait_ge(w_ld["proj"], 16 * 7)
            pe.wait_ge(setup_dve, 3)
            wa, wb, wta, wtb = wp_src[0], wp_src[1][0:CB, :], wp_src[2], wp_src[3][0:CB, :]
            for b, rows, la, lb in ((0, P, wa[:, 0:P], wb[:, 0:P]), (1, CB, wa[:, P:C], wb[:, P:C]),
                                    (3, P, bp_row[:, 0, :], bp_row[0:CB, 1, :])):
                t.matmul(bank(b)[0:rows, 0:C], la, wta[:, :], start=True, stop=False)
                last = t.matmul(bank(b)[0:rows, 0:C], lb, wtb, start=False, stop=True)
            last.then_inc(setup_pe, 1)
            pe.sem_inc(setup_ready, 1)

            with pe.Fori(0, B) as i:
                start_image(pe, i)

                def conv(h):
                    p = h // 2
                    if p >= 2 and h % 2 == 0:
                        pe.wait_ge(ring_ld[p], RING)
                    if h >= 2:
                        pe.wait_ge(conv_sb, h - 1)
                    for nh in range(QC):
                        for s in range(2):
                            rhs = ring[p % 2][s][0:KROWS[s], h % 2, :].rearrange(
                                "p (a b) -> p a b", b=PW)[:, SH // QC * nh:SH // QC * (nh + 1), 0:SW]
                            last = t.matmul(bank(2 * (h % 2) + nh)[0:CM, :], wconv[s][0:KROWS[s], h, :], rhs,
                                            start=s == 0, stop=s == 1)
                    last.then_inc(conv_ps, 1)

                def conv_transposes(h):
                    pe.wait_ge(conv_sb, h + 1)
                    if h >= 2:
                        pe.wait_ge(qkT_sb, h - 1)
                    for k in range(NC):
                        last = t.transpose(bank(4 + h % 2)[:, 64 * k:64 * k + 56],
                                           qkve[h % 2][0:56, P * k:P * (k + 1)], ident[0:56, 0:56])
                    last.then_inc(qkT_ps, 1)

                for h in range(NH):
                    conv(h)
                    if h:
                        conv_transposes(h - 1)
                conv_transposes(NH - 1)
                pe.wait_ge(qkT_sb, NH)
                for f in range(2):
                    ch = slice(HALF * f, HALF * (f + 1))
                    for k in range(NC):
                        last = t.matmul(bank(6 + f)[0:HALF, 0:HALF], qkt[:, k, 1, ch], qkt[:, k, 0, ch],
                                        start=k == 0, stop=k == NC - 1)
                    last.then_inc(logit_ps, 1)
                for f in range(2):
                    pe.wait_ge(attn_sb, f + 1)
                    t.transpose(bank(6 + f)[0:HALF, P:P + HALF], lm[:, f, :], ident[0:HALF, 0:HALF]).then_inc(attnT_ps, 1)
                for f in range(2):
                    pe.wait_ge(attnT_sb, f + 1)
                    t.matmul(bank(6 + f)[0:HALF, 2 * P:2 * P + C], attn_t[:, f, :], wf_t[:, f, :],
                             start=True, stop=True).then_inc(mix_ps, 1)
                pe.wait_ge(mix_sb, 2)
                for p in range(2):
                    pe.wait_ge(v_dma[p], 16 * NH // 2)
                for k in range(NC):
                    if k >= 4:
                        pe.wait_ge(y_sb, k - 3)
                    o = bank(k % 4)
                    for f in range(2):
                        t.matmul(o[:, 0:C], vp[:, f, P * k:P * (k + 1)], mix[:, f, :], start=f == 0, stop=False,
                                 skip_group_check=True)
                    for f in range(2):
                        last = t.matmul(o[:, HALF * f:HALF * (f + 1)], xn[:, f, P * k:P * (k + 1)],
                                        ident[0:HALF, 0:HALF], start=False,
                                        stop=f == 1, skip_group_check=True)
                    last.then_inc(y_ps, 1)

                def norm_transposes(norm):
                    for j in range(QC):
                        pe.wait_ge(xhat_sb, NC * norm + TPC * (j + 1))
                        for b, c0 in ((j, 0), (2 + j, P)):
                            for kk in range(TPC):
                                last = t.transpose(bank(b)[:, P * kk:P * (kk + 1)],
                                                   xhat[:, TPC * j + kk, c0:c0 + P], ident[:, :])
                            last.then_inc(lnT_ps, 1)

                norm_transposes(0)

                def parts(wa_hi, wa_lo, wb_hi, wb_lo):
                    return ((T0, wa_hi), (T0, wa_lo), (T2, wa_hi), (T1, wb_hi), (T1, wb_lo))

                qkv = parts(wqa_hi, wqa_lo, wqb_hi, wqb_lo)
                for n in range(6):
                    f, nh = n % 3, n // 3
                    if f == 0:
                        pe.wait_ge(T_lo, 2 * (nh + 1))
                        pe.wait_ge(T_hi, 2 * (nh + 1))
                    if n >= 4:
                        pe.wait_ge(qk_lo, n - 3)
                    for m, (act_part, w_part) in enumerate(qkv):
                        last = t.matmul(bank(4 + n % 4), w_part[:, P * f:P * (f + 1)],
                                        act_part[:, BANK * nh:BANK * (nh + 1)], start=m == 0, stop=m == 4)
                    last.then_inc(qk_ps, 1)
                for k in range(NC):
                    if k >= 4:
                        pe.wait_ge(v_done, k - 3)
                    for m, (act_part, w_part) in enumerate(qkv):
                        last = t.matmul(bank(k % 4)[:, 0:C], act_part[:, P * k:P * (k + 1)],
                                        w_part[:, 2 * C:3 * C], start=m == 0, stop=m == 4)
                    last.then_inc(v_ps, 1)

                pe.wait_ge(v_done, NC)
                pe.wait_ge(qk_lo, 6)

                def transposed_maxima(g, b):
                    pe.wait_ge(mneg_sb, g + 1)
                    for qc in range(NC):
                        last = t.matmul(bank(b + qc // 4)[0:2 * len(GROUPS[g]), P * (qc % 4):P * (qc % 4 + 1)],
                                        mneg[g][:, qc, :, :].rearrange("p h r -> p (h r)"), ident_r[:, :],
                                        start=True, stop=True)
                    last.then_inc(mT_ps, 1)

                for h in range(H):
                    pe.wait_ge(stack_ld[h], 16 * 6)
                    for qc in range(NC):
                        n = NC * h + qc
                        r = n if n < M0_SLOT else n + 1
                        if r >= 4:
                            if r - 4 == M0_SLOT:
                                pe.wait_ge(mrow_sb, 1)
                            else:
                                pe.wait_ge(mx_sb, (r - 4 if r - 4 < M0_SLOT else r - 5) + 1)
                        keys = P * (qc + 1)
                        o = bank(2 * (r % 4), 2)
                        for k0 in range(0, keys, BANK):
                            k1 = min(keys, k0 + BANK)
                            t.matmul(o[:, k0:k1], QS[0:96, h, P * qc:P * (qc + 1)], KS[0:96, h, k0:k1],
                                     start=True, stop=k1 < keys, skip_group_check=True)
                        t.matmul(o[:, P * qc:keys], ident_bf[:, :], keep_q[:, :], start=False, stop=True,
                                 skip_group_check=True).then_inc(s_ps, 1)
                    if n == M0_SLOT - 1:
                        pe.wait_ge(mx_sb, n - 2)
                        transposed_maxima(0, 2 * (M0_SLOT % 4))
                pe.wait_ge(mx_sb, NC * H)
                transposed_maxima(1, 2)
                pe.wait_ge(ks_ones, 1)

                def scores(s, tile):
                    g, c, kb = STEPS[s]
                    h = GROUPS[g][tile]
                    q = first_tile[s] + tile
                    off, w = query_range(c, kb)
                    if q >= 4:
                        pe.wait_ge(p_sb, q - 3)
                    if c == 0 and kb == 0 and tile == 0:
                        pe.wait_ge(m_ld[g], 16 * len(GROUPS[g]))
                    diagonal = kb >= TPC * c
                    last = t.matmul(bank(4 + q % 4)[:, 0:w], KS[0:98, h, P * kb:P * (kb + 1)],
                                    QS[0:98, h, BANK * c + off:BANK * (c + 1)], start=True, stop=not diagonal,
                                    skip_group_check=True)
                    if diagonal:
                        last = t.matmul(bank(4 + q % 4)[:, 0:P], ident_bf[:, :], keep_k[:, :], start=False, stop=True,
                                        skip_group_check=True)
                    last.then_inc(st_ps, 1)

                def values(s):
                    g, c, kb = STEPS[s]
                    heads = GROUPS[g]
                    off, w = query_range(c, kb)
                    first, end = kb == 0, kb == TPC * (c + 1) - 1
                    if first and g == 0 and c == 1:
                        pe.wait_ge(mrow_sb, 2)
                    if first and g == 1:
                        pe.wait_ge(at_sb, c + 1)
                    pe.wait_ge(p_sb, first_tile[s] + len(heads))
                    b_sum, row0 = (2 * c + 1, 0) if g == 0 else (2 * c, 64)
                    for kind in range(2):
                        for j, h in enumerate(heads):
                            q = first_tile[s] + j
                            if kind == 0:
                                o, w_ap = bank(2 * c)[D * j:D * (j + 1), off:BANK], v_sb[:, kb, D * h:D * (h + 1)]
                            else:
                                o, w_ap = bank(b_sum)[row0 + D * j:row0 + D * (j + 1), off:BANK], ones32[:, :]
                            last = t.matmul(o, w_ap, PT[:, q % 8, 0:w], start=first, stop=end, skip_group_check=True)
                    last.then_inc(p_used, 1)

                for s in range(len(STEPS) + 1):
                    if s < len(STEPS):
                        for tile in range(len(GROUPS[STEPS[s][0]])):
                            scores(s, tile)
                    if s:
                        values(s - 1)
                pe.wait_ge(p_sb, len(step_of_tile))
                pe.wait_ge(at_sb, 2 * QC)
                for k in range(NC):
                    if k >= 4:
                        pe.wait_ge(o_sb, k - 3)
                    o = bank(4 + k % 4)[:, 0:C]
                    t.matmul(o, aTa[:, P * k:P * (k + 1)], w2pa[:, :], start=True, stop=False)
                    t.matmul(o, aTb[:, P * k:P * (k + 1)], w2pb[:, :], start=False, stop=True).then_inc(o_ps, 1)

                norm_transposes(1)

                def gate_scores():
                    for k in range(NC):
                        for m, (act_part, w_part) in enumerate(parts(wga_hi, wga_lo, wgb_hi, wgb_lo)):
                            last = t.matmul(bank(7)[:, E * k:E * (k + 1)], act_part[:, P * k:P * (k + 1)], w_part[:, :],
                                            start=m == 0, stop=m == 4)
                    last.then_inc(gate_ps, 1)

                def up(n):
                    c, e, j = n // (E * J), n // J % E, n % J
                    if n >= 2:
                        pe.wait_ge(gelu_sb, n - 1)
                    for m, (act_part, w_part) in enumerate(parts(w1a_hi, w1a_lo, w1b_hi, w1b_lo)):
                        last = t.matmul(bank(n % 2), w_part[:, HID * e + P * j:HID * e + P * (j + 1)],
                                        act_part[:, BANK * c:BANK * (c + 1)], start=m == 0, stop=m == 4)
                    last.then_inc(up_ps, 1)

                def down(n):
                    idx, j = n // J, n % J
                    e = idx % E
                    if j == 0 and idx >= 2:
                        pe.wait_ge(t_acc, added(idx - 2))
                    if n == 0:
                        pe.wait_ge(o_sb, NC)
                    if n == J:
                        pe.wait_ge(gsub, 1)
                    pe.wait_ge(gelu_sb, n + 1)
                    pe.wait_ge(lo_sb, n + 1)
                    for tt in range(TPC):
                        o = bank(4 + 2 * (idx % 2) + tt // 2)[:, C * (tt % 2):C * (tt % 2 + 1)]
                        for m, (h_part, w_part) in enumerate(((g_hi, w2_hi), (g_hi, w2_lo), (g_lo, w2_hi))):
                            last = t.matmul(o, h_part[:, n % 2, P * tt:P * (tt + 1)], w_part[:, e * J + j, :],
                                            start=j == 0 and m == 0 and tt % 2 == 0, stop=j == J - 1 and m == 2,
                                            skip_group_check=True)
                    last.then_inc(down_ps, 1)

                def out_transposes(c):
                    pe.wait_ge(t_acc, added(E * (c + 1) - 1))
                    if c:
                        pe.wait_ge(out_sb, 2 * c)
                    for b, c0, rows in ((2, 0, P), (3, P, CB)):
                        for kk in range(TPC):
                            last = t.transpose(bank(b)[0:rows, P * kk:P * (kk + 1)], t_sb[:, TPC * c + kk, c0:c0 + rows],
                                               ident[:, :])
                        last.then_inc(outT_ps, 1)

                pe.wait_ge(T_lo, 8)
                pe.wait_ge(T_hi, 8)
                up(0)
                gate_scores()
                for n in range(NT):
                    if n + 1 < NT:
                        up(n + 1)
                    down(n)
                    if n == 9:
                        average_mean(pe)
                    if n == 11:
                        average_var(pe)
                    if n == OUT0:
                        out_transposes(0)
                out_transposes(1)


def kernel(**inputs):
    import numpy as np
    import concourse.bacc as bacc
    from concourse.bass_utils import run_bass_kernel_spmd

    a = {k: np.asarray(v) for k, v in inputs.items()}
    f = np.float32
    nh, hc = a["L0_conv_bq_p"].shape
    kinds = "qkv"

    def per_kind(parts):
        pad = np.zeros(parts[0].shape[:-1] + (32 - hc,), f)
        return np.ascontiguousarray(np.concatenate([parts[0], pad, parts[1], pad, parts[2]], axis=-1))

    conv_w = per_kind([a[f"L0_conv_w{k}_p"].transpose(2, 0, 1) for k in kinds])
    conv_bias_row = per_kind([a[f"L0_conv_b{k}_p"] for k in kinds])
    conv_taps = per_kind([a[f"L0_conv_w{k}_d"].reshape(nh, hc, 9).transpose(2, 0, 1) for k in kinds])
    conv_bias = np.ascontiguousarray(per_kind([a[f"L0_conv_b{k}_d"].reshape(nh, hc) for k in kinds]).T)
    alpha_rows = np.ascontiguousarray(np.repeat(a["L0_conv_alpha"], hc).reshape(2, -1).T)
    w = a["L1_attn_W_qkv"].reshape(6, 3, -1, a["L1_attn_W_qkv"].shape[1])
    c = w.shape[-1]
    k_, q_, v_ = (w[:, n].reshape(-1, c) for n in range(3))
    w_qkv = np.concatenate([q_[:128], k_[:128], q_[128:], k_[128:], v_]).T

    def ab(m):
        return np.ascontiguousarray(m[:128]), np.ascontiguousarray(np.concatenate([m[128:], m[128:]]))

    w_qkv_a, w_qkv_b = ab(w_qkv)
    gate_a, gate_b2 = ab(a["L1_ffn_gate_w"])
    w1_a, w1_b = ab(a["L1_ffn_w1"].transpose(1, 0, 2).reshape(c, -1))
    e, hid, _ = a["L1_ffn_w2"].shape
    arrays = {
        "x": a["x"], "ln_g": a["L0_conv_ln_g"], "ln_b": a["L0_conv_ln_b"],
        "conv_w": conv_w, "conv_bias_row": conv_bias_row, "conv_taps": conv_taps, "conv_bias": conv_bias,
        "alpha_rows": alpha_rows, "w_f_t": a["L0_conv_w_f"].T, "b_f": a["L0_conv_b_f"],
        "w_qkv_a": w_qkv_a, "w_qkv_b": w_qkv_b,
        "w_proj": a["L1_attn_W_proj"], "w_proj_t": a["L1_attn_W_proj"].T, "b_proj": a["L1_attn_b_proj"],
        "gate_w_a": gate_a, "gate_w_b": gate_b2, "gate_b": a["L1_ffn_gate_b"],
        "w1_a": w1_a, "w1_b": w1_b, "b1_t": a["L1_ffn_b1"].reshape(e * hid // 128, 128).T,
        "w2": a["L1_ffn_w2"].reshape(e * hid // 128, 128, c).transpose(1, 0, 2), "b2": a["L1_ffn_b2"],
    }
    arrays = {k: np.ascontiguousarray(v) for k, v in arrays.items()}
    nc = bacc.Bacc("TRN2", target_bir_lowering=False, num_devices=1, dynamic_dma_scratch_size=1024)
    aps = [nc.dram_tensor(k, v.shape, mybir.dt.from_np(v.dtype), kind="ExternalInput").ap() for k, v in arrays.items()]
    out = nc.dram_tensor("out", a["x"].shape, F32, kind="ExternalOutput").ap()
    hybrid_block_kernel(nc, *aps, out)
    r = run_bass_kernel_spmd(nc, [arrays], core_ids=[0])
    return r.results[0]["out"]
```

```python
from contextlib import ExitStack

import concourse.bass as bass
from concourse import mybir

F32 = mybir.dt.float32
F32R = mybir.dt.float32r
BF16 = mybir.dt.bfloat16
ALU = mybir.AluOpType
ACT = mybir.ActivationFunctionType
AX = mybir.AxisListType.X

NEG = -3.0e38
P = 128
BANK = 512


def hybrid_block_kernel(nc, x, ln_g, ln_b, conv_w, conv_bias_row, conv_taps, conv_bias, alpha_rows, w_f_t, b_f,
                        w_qkv_a, w_qkv_b, w_proj, w_proj_t, b_proj, gate_w_a, gate_w_b, gate_b, w1_a, w1_b, b1_t,
                        w2, b2, out):
    B, C, SH, SW = x.shape
    N = SH * SW
    NC = N // P
    HALF = C // 2
    NH, HC = conv_w.shape[1], conv_w.shape[0]
    HPH = NH // 2
    CM = conv_w.shape[2]
    PW = SW + 2
    XP = 1160
    SL = SH * PW
    TAPS = [3 * dy + dx for dy in range(3) for dx in range(3)]
    SHIFT = [PW * dy + dx for dy in range(3) for dx in range(3)]
    STACKS = [TAPS[:5], TAPS[5:]]
    KROWS = [(HC + 1) * len(s) for s in STACKS]
    H, D = 6, C // 6
    GROUPS = [[0, 1], [2, 3], [4, 5]]
    SCALE = float(D) ** -0.5
    E = gate_w_a.shape[1]
    HID = w1_a.shape[1] // E
    J = HID // P
    CB = C - P
    QC = N // BANK
    TPC = BANK // P
    NT = QC * E * J
    assert (N, C, CB, QC, HC * NH) == (1024, 192, 64, 2, C) and KROWS[0] <= P

    scratch = nc.dram_tensor("padded_scratch", [C, XP], F32, kind="Internal").ap()
    inside_taps = nc.dram_tensor("inside_taps", [len(TAPS), SL], F32, kind="Internal").ap()
    mask_scratch = nc.dram_tensor("inside_scratch", [XP], F32, kind="Internal").ap()

    with ExitStack() as ctx:
        base = (nc.sbuf_base + 31) // 32 * 32
        place = [0]

        def at(name, shape, dt, offset):
            return nc.alloc_sbuf_tensor_at(name, shape, dt, offset=base + offset)

        def size(shape, dt):
            n = 1
            for s in shape[1:]:
                n *= s
            return (n * (2 if dt == BF16 else 4) + 31) // 32 * 32

        def sb(name, shape, dt=F32):
            t = at(name, shape, dt, place[0])
            place[0] += size(shape, dt)
            return t

        def sb_split(name, shape):
            hi = sb(name + "_hi", shape, F32R)
            src = at(name + "_src", shape, F32, place[0])
            lo = sb(name + "_lo", shape, F32R)
            return hi, lo, src

        w1a_hi, w1a_lo, w1a_src = sb_split("w1a", [P, E * HID])
        w1b_hi, w1b_lo, w1b_src = sb_split("w1b", [P, E * HID])
        w2_parts = sb("w2_parts", [P, E * J, 2, C], F32R)
        wqa_hi, wqa_lo, wqa_src = sb_split("wqkv_a", [P, 3 * C])
        wqb_hi, wqb_lo, wqb_src = sb_split("wqkv_b", [P, 3 * C])
        wga_hi, wga_lo, wga_src = sb_split("wgate_a", [P, E])
        wgb_hi, wgb_lo, wgb_src = sb_split("wgate_b", [P, E])
        wconv = [sb(f"wconv{s}", [P, NH, CM]) for s in range(2)]
        wf_t = sb("wf_t", [HALF, 2, C])
        w2pa = sb("wproj2_a", [P, C])
        w2pb = sb("wproj2_b", [CB, C])
        b2p_bc = sb("bproj2_bc", [P, C])
        bf_bc = sb("bf_bc", [P, C])
        gb_bc = sb("gate_b_bc", [P, E])
        b1_sb = sb("b1_sb", [P, E * J])
        convb = sb("convb", [CM, NH])
        ralpha = sb("ralpha", [HALF, 2])
        ident = sb("ident", [P, P])
        ident_r = sb("ident_r", [P, P], F32R)
        ident_bf = sb("ident_bf", [P, P], BF16)
        keep_q = sb("mask_rows_q", [P, P], BF16)
        keep_k = sb("mask_rows_k", [P, P], BF16)
        block_mask = sb("block_mask", [HALF, HALF])
        ones_avg = sb("ones_avg", [HALF, HALF])
        ones32 = sb("ones32", [P, D])
        before = sb("before", [P, E, E])
        minus_half = sb("minus_half", [P, 8])
        pstat = sb("pstat", [HALF, 4, 6])
        pmv = sb("pmv", [HALF, 2])
        img = sb("img", [HALF, 8])
        lm = sb("lm", [HALF, 2, HALF])
        attn_t = sb("attn_t", [HALF, 2, HALF])
        mix = sb("mix", [HALF, 2, C])
        sm = sb("sm", [HALF, 8])
        tstat = sb("tstat", [P, NC, 6])
        tmv = sb("tmv", [P, NC, 2])
        rstd = sb("rstd", [P, 2, NC])
        mx = sb("mx", [P, NC, H])
        mx_far = sb("mx_far", [P, NC, H])
        mneg = [sb(f"mneg{g}", [P, NC, len(hs), 2], F32R) for g, hs in enumerate(GROUPS)]
        gs = sb("gs", [P, NC, E])
        gx = sb("gx", [P, NC, E])
        gcmp = sb("gcmp", [P, NC, E, E])
        geq = sb("geq", [P, NC, E, E])
        gsum = sb("gsum", [P, NC, 4])
        gate = sb("gate", [P, NC, E])
        t_sb = sb("t_sb", [P, NC, C])
        xn_at = place[0]
        xn = sb("xn", [HALF, 2, N])
        v_sb = at("v_sb", [P, NC, C], F32, xn_at)
        R_T = place[0]
        T0 = sb("T0_hi", [P, N], F32R)
        T1 = sb("T1", [P, N], F32R)
        T2 = sb("T2_lo", [P, N], F32R)
        sums1 = sb("sums1", [P, BANK])
        unscaled = [sb(f"unscaled{g}", [P, BANK]) for g in range(2)]
        mrow = [sb("mrow0", [2 * len(GROUPS[0]), N], F32R)]
        mrow += [at(f"mrow{g}", [2 * len(GROUPS[g]), N], F32R, R_T + 4096 * g) for g in (1, 2)]
        R = place[0]
        K = 1024
        ring = [[at(f"ring{s}_{k}", [P, 2, SL], F32, R + s * 17408 + k * 8704) for k in range(2)] for s in range(2)]
        xhat = at("xhat", [P, NC, 2 * P], F32, R)
        QS = at("QS", [P, H, N], F32R, R)
        KS = at("KS", [P, H, N], F32R, R + 24 * K)
        x_sb = at("x_sb", [HALF, 2, N], F32, R + 34 * K)
        qkve = [at(f"qkve{s}", [CM, N], F32, R + 34 * K + 4 * K * s) for s in range(2)]
        xpad = at("xpad", [HALF, 2, XP], F32, R + 34 * K)
        gb_sb = at("gb_sb", [HALF, 2, N], F32, R + 42 * K)
        qkt = at("qkt", [P, NC, 2, C], F32, R + 42 * K)
        QKh = at("QKh", [P, 3, N], F32R, R + 48 * K)
        QKl = at("QKl", [P, 3, N], F32R, R + 60 * K)
        aTa = at("aTa", [P, N], F32, R + 24 * K)
        aTb = at("aTb", [CB, N], F32, R + 28 * K)
        vp = at("vp", [HALF, 2, N], F32, R + 54 * K)
        PT = at("PT", [P, 8, BANK], F32, R + 56 * K)
        g32 = at("g32", [P, 2, BANK], F32, R + 50 * K)
        g_hi = at("g_hi", [P, 2, BANK], F32R, R + 54 * K)
        g_lo = at("g_lo", [P, 2, BANK], F32R, R + 58 * K)
        b2_bc = at("b2_bc", [P, E, C], F32, R + 62 * K)
        outs_a = at("outs_a", [P, QC, BANK], F32, R + 65 * K)
        outs_b = at("outs_b", [CB, QC, BANK], F32, R + 69 * K)
        sums = [at("sums0", [P, BANK], F32, R + 72 * K), sums1]
        w2_src = at("w2_src", [P, E * J, C], F32, R)
        grow = at("grow", [E, QC, BANK], F32, R + 65 * K)
        wp_src = [at(f"wp_src{i}", [P, C], F32, R + 65 * K + 768 * i) for i in range(4)]
        bp_src = at("bp_src", [P, 2], F32, R + 69 * K)
        bp_row = at("bp_row", [P, 2, P], F32, R + 70 * K)
        bpb = at("bpb", [P, C], F32, R + 72 * K)
        wtap = [at(f"wtap{s}", [P, NH, CM], F32, R + 54 * K + 3 * K * s) for s in range(2)]
        inside = at("inside", [1, XP], F32, R + 60 * K)
        ctx.enter_context(nc.sbuf_tensor("whole_map", [P, (R + 75 * K) // 4], F32))
        ps = ctx.enter_context(nc.psum_tensor("ps", [P, 8 * BANK], F32))

        def bank(b, n=1):
            return ps[:, b * BANK:(b + n) * BANK]

        names = []

        def sem(name):
            s = ctx.enter_context(nc.semaphore(name))
            names.append(s)
            return s

        conv_ps, qkT_ps, logit_ps, attnT_ps, mix_ps, y_ps = map(sem, "conv_ps qkT_ps logit_ps attnT_ps mix_ps y_ps".split())
        lnT_ps, qk_ps, v_ps, s_ps, mT_ps, st_ps, p_used, o_ps = map(
            sem, "lnT_ps qk_ps v_ps s_ps mT_ps st_ps p_used o_ps".split())
        gate_ps, gateT_ps, up_ps, down_ps, last_pair_ps, stat_ps, outT_ps = map(
            sem, "gate_ps gateT_ps up_ps down_ps last_pair_ps stat_ps outT_ps".split())
        conv_sb, e_sb, mix_sb, T_hi, qk_hi, v_done, mrow_sb, p_sb, unscaled_sb, grow_sb, gexp_sb, gelu_sb, out_sb = map(
            sem, "conv_sb e_sb mix_sb T_hi qk_hi v_done mrow_sb p_sb unscaled_sb grow_sb gexp_sb gelu_sb out_sb".split())
        chain, qkT_sb, lm_sb, attn_sb, attnT_sb, y_sb, veps, xhat_sb, T_lo, qk_lo, mx_sb, mneg_sb, at_sb, o_sb = map(
            sem, "chain qkT_sb lm_sb attn_sb attnT_sb y_sb veps xhat_sb T_lo qk_lo mx_sb mneg_sb at_sb o_sb".split())
        gsub, lo_sb, t_acc, xstat, img_veps, xg_sb, xn_sb = map(
            sem, "gsub lo_sb t_acc xstat img_veps xg_sb xn_sb".split())
        rstd_sb, tb_sb, ks_ones, img_rstd, pad_zero, padded = map(sem, "rstd_sb tb_sb ks_ones img_rstd pad_zero padded".split())
        ring_ld = [sem(f"ring_ld{p}") for p in range(4)]
        v_dma = [sem(f"v_dma{p}") for p in range(2)]
        stack_ld = [sem(f"stack_ld{n}") for n in range(4)]
        STACK_LOADS = 16 * 6
        m_ld = [[sem(f"m_ld{g}_{half}") for half in range(QC)] for g in range(len(GROUPS))]
        b2_ld, x_ld, g_ld, b_ld, scr_w = map(sem, "b2_ld x_ld g_ld b_ld scr_w".split())
        started = sem("started")
        per_image = range(names[0].num, names[-1].num + 1)
        assert [s.num for s in names] == list(per_image)
        next_image, dram_written = map(sem, "next_image dram_written".split())
        w_ld = {k: sem("w_ld_" + k) for k in "conv small proj gate qkv w1a w1b w2 inside".split()}
        setup_pool, inside_zero, setup_dve, w2_split, setup_pe, setup_ready = map(
            sem, "setup_pool inside_zero setup_dve w2_split setup_pe setup_ready".split())
        RING = [16 * (len(TAPS) + (len(STACKS) if p < 2 else 0)) for p in range(4)]

        block = ctx.enter_context(nc.Block())

        def load_ring(sp, p):
            for s, taps in enumerate(STACKS):
                dst = ring[p % 2][s]
                for j, tap in enumerate(taps):
                    src = scratch[2 * p * HC:2 * (p + 1) * HC, SHIFT[tap]:SHIFT[tap] + SL]
                    sp.dma_start(dst[HC * j:HC * (j + 1), :, :],
                                 src.rearrange("(h c) l -> c h l", c=HC)).then_inc(ring_ld[p], 16)
                if p >= 2:
                    continue
                nt = len(taps)
                sp.dma_start(dst[HC * nt:HC * nt + nt, :, :],
                             inside_taps[taps[0]:taps[0] + nt, :].unsqueeze(1).to_broadcast([nt, 2, SL])
                             ).then_inc(ring_ld[p], 16)

        def load_image(sp, i):
            sp.dma_start(x_sb[:, :, :], x[i].rearrange("(h p) a b -> p h (a b)", h=2)).then_inc(x_ld, 16)
            sp.dma_start(gb_sb[:, :, :], ln_g.rearrange("(h p) a b -> p h (a b)", h=2)).then_inc(g_ld, 16)

        def load_shift(sp):
            sp.wait_ge(xg_sb, 2)
            sp.dma_start(gb_sb[:, :, :], ln_b.rearrange("(h p) a b -> p h (a b)", h=2)).then_inc(b_ld, 16)

        def store_padded(sp):
            sp.wait_ge(padded, 2)
            sp.dma_start(scratch.rearrange("(h p) l -> p h l", h=2), xpad[:, :, :]).then_inc(scr_w, 16)
            sp.wait_ge(scr_w, 16)

        def chained(dve):
            count = [0]

            def link(ins):
                count[0] += 1
                ins.then_inc(chain, 1)
                dve.wait_ge(chain, count[0])
            return link

        def image_norm_steps(dve, link):
            v = nc.vector

            def stats(q):
                if q == 0:
                    dve.wait_ge(x_ld, 16)
                ins = v.bn_stats(pstat[:, q, :], x_sb[:, q // 2, BANK * (q % 2):BANK * (q % 2 + 1)])
                if q == 3:
                    link(ins)

            def partition_mean():
                v.bn_aggr(pmv[:, :], pstat[:, :, :]).then_inc(xstat, 1)

            def deviation():
                dve.wait_ge(xstat, 1)
                dve.wait_ge(stat_ps, 1)
                link(v.tensor_copy(img[:, 0:1], bank(stat_bank)[0:HALF, 0:1]))
                link(v.tensor_tensor(img[:, 1:2], pmv[:, 0:1], img[:, 0:1], ALU.subtract))
                link(v.tensor_tensor(img[:, 2:3], img[:, 1:2], img[:, 1:2], ALU.mult))
                v.tensor_tensor(img[:, 3:4], img[:, 2:3], pmv[:, 1:2], ALU.add).then_inc(xstat, 1)

            def variance():
                dve.wait_ge(stat_ps, 2)
                v.tensor_scalar(img[:, 4:5], bank(stat_bank)[0:HALF, 1:2], 1e-5, None, ALU.add).then_inc(img_veps, 1)

            def gain(h):
                if h == 0:
                    dve.wait_ge(g_ld, 16)
                v.scalar_tensor_tensor(out=x_sb[:, h, :], in0=x_sb[:, h, :], scalar=img[:, 0:1],
                                       in1=gb_sb[:, h, :], op0=ALU.subtract, op1=ALU.mult).then_inc(xg_sb, 1)

            def shift(h):
                if h == 0:
                    dve.wait_ge(b_ld, 16)
                    dve.wait_ge(img_rstd, 1)
                    dve.wait_ge(xg_sb, 2)
                v.scalar_tensor_tensor(out=xn[:, h, :], in0=x_sb[:, h, :], scalar=img[:, 5:6], in1=gb_sb[:, h, :],
                                       op0=ALU.mult, op1=ALU.add).then_inc(xn_sb, 1)

            return stats, partition_mean, deviation, variance, gain, shift

        def start_image(eng, i):
            eng.wait_ge(next_image, i + 1)
            eng.sem_inc(started, 1)

        def average_mean(pe):
            pe.wait_ge(xstat, 1)
            nc.tensor.matmul(bank(stat_bank)[0:HALF, 0:1], ones_avg[:, :], pmv[:, 0:1], start=True, stop=True).then_inc(stat_ps, 1)

        def average_var(pe):
            pe.wait_ge(xstat, 2)
            nc.tensor.matmul(bank(stat_bank)[0:HALF, 1:2], ones_avg[:, :], img[:, 3:4], start=True, stop=True).then_inc(stat_ps, 1)

        def image_rstd(pool):
            pool.wait_ge(img_veps, 1)
            nc.gpsimd.tensor_tensor(img[:, 5:6], img[:, 4:5], minus_half[0:HALF, 0:1], ALU.pow).then_inc(img_rstd, 1)

        def pad_image(pool):
            pool.wait_ge(xn_sb, 2)
            nc.gpsimd.memset(xpad[:, :, :], 0.0).then_inc(pad_zero, 1)
            pool.wait_ge(pad_zero, 1)
            for h in range(2):
                inner = xpad[:, h, 0:PW * (SH + 2)].rearrange("p (a b) -> p a b", b=PW)[:, 1:SH + 1, 1:SW + 1]
                nc.gpsimd.tensor_copy(inner, xn[:, h, :].rearrange("p (a b) -> p a b", b=SW)).then_inc(padded, 1)

        STEPS = [(g, c, kb) for g in range(len(GROUPS)) for c in range(QC) for kb in range(TPC * (c + 1))]
        def half_done(g, c):
            return max(s for s, (gg, cc, _) in enumerate(STEPS) if (gg, cc) == (g, c)) + 1

        def query_range(c, kb):
            off = P * (kb - TPC * c) if kb >= TPC * c else 0
            return off, BANK - off

        PIECES, DUE = [], []
        for g, heads in enumerate(GROUPS):
            for half in range(QC):
                PIECES += [(h, qc, k0, min(BANK, P * (qc + 1) - k0)) for h in heads
                           for qc in range(TPC * half, TPC * (half + 1)) for k0 in range(0, P * (qc + 1), BANK)]
                DUE.append((g, half, len(PIECES)))
        LAST_PIECE = {n - 1: (g, half) for g, half, n in DUE}
        SG = len(STEPS) // len(GROUPS)
        LEAD = 0
        BEHIND = 2
        PIECES_PER_STEP = 2

        def pass1_schedule():
            before_steps, at_step, due, n = [], [[] for _ in STEPS], list(DUE), 0
            for uses, more in [(before_steps, DUE[QC - 1][2] + LEAD)] + [(uses, PIECES_PER_STEP) for uses in at_step]:
                if n == len(PIECES) and due:
                    uses.append(("maxima", *due.pop(0)[:2]))
                for _ in range(min(more, len(PIECES) - n)):
                    uses.append(("scores", n))
                    n += 1
                    if due and n >= due[0][2] + BEHIND:
                        uses.append(("maxima", *due.pop(0)[:2]))
            return before_steps, at_step

        PASS1_BEFORE, PASS1_AT = pass1_schedule()
        SLOTS = PASS1_BEFORE + [use for uses in PASS1_AT for use in uses]
        SLOT_BANK = {use: n % 4 if n < len(PASS1_BEFORE) else n % 2 for n, use in enumerate(SLOTS)}

        QK_ORDER = [(0, 0), (1, 0), (0, 1), (2, 0), (1, 1), (2, 1)]
        QK_FIRST = 1
        LAST_GROUP = len(GROUPS) - 1
        AT_GROUP = QC * LAST_GROUP
        OUT_STEP = SG * LAST_GROUP + 9

        def out_bank(k):
            return k % 2 if k < TPC else 6 + k % 2


        OUT0 = 32
        STAT = 13
        BIAS0 = 8

        def acc_bank(idx, tt):
            return 2 + (TPC * idx + tt) % 6

        stat_use = (STAT // J + 1, 0)
        stat_bank = acc_bank(*stat_use)
        out_use = [(OUT0 // J + 1, 0), (OUT0 // J + 1, 1), (QC * E, 0), (QC * E, 1)]

        T_ORDER = []
        for n in range(NT + 2):
            if n >= J and n % J < 2:
                T_ORDER += [("sum", n // J - 1, 2 * (n % J) + tt, part) for part in (0, 1) for tt in (0, 1)]
            if BIAS0 <= n < BIAS0 + NC * E:
                T_ORDER.append(("bias", n - BIAS0))

        def t_count(*op):
            return T_ORDER.index(op) + 1

        @block.sync
        def _(sp):
            load_image(sp, 0)
            sp.dma_start(wp_src[0][0:P, :], w_proj[0:P, :]).then_inc(w_ld["proj"], 16)
            sp.dma_start(wp_src[1][0:CB, :], w_proj[P:C, :]).then_inc(w_ld["proj"], 16)
            sp.dma_start(wp_src[2][0:P, :], w_proj_t[0:P, :]).then_inc(w_ld["proj"], 16)
            sp.dma_start(wp_src[3][0:CB, :], w_proj_t[P:C, :]).then_inc(w_ld["proj"], 16)
            sp.dma_start(bp_src[:, 0:1], b_proj[0:P].rearrange("(p a) -> p a", a=1)).then_inc(w_ld["proj"], 16)
            sp.dma_start(bp_src[0:CB, 1:2], b_proj[P:C].rearrange("(p a) -> p a", a=1)).then_inc(w_ld["proj"], 16)
            sp.dma_start(bpb[:, :], b_proj.partition_broadcast(P)).then_inc(w_ld["proj"], 16)
            sp.dma_start(bf_bc[:, :], b_f.partition_broadcast(P)).then_inc(w_ld["small"], 16)
            sp.dma_start(gb_bc[:, :], gate_b.partition_broadcast(P)).then_inc(w_ld["small"], 16)
            sp.dma_start(b1_sb[:, :], b1_t).then_inc(w_ld["small"], 16)
            sp.dma_start(convb[:, :], conv_bias).then_inc(w_ld["small"], 16)
            sp.dma_start(wf_t[:, :, :], w_f_t.rearrange("(h p) o -> p h o", h=2)).then_inc(w_ld["small"], 16)
            sp.dma_start(ralpha[:, :], alpha_rows).then_inc(w_ld["small"], 16)
            sp.wait_ge(setup_pool, 2)
            sp.dma_start(mask_scratch.rearrange("(a l) -> a l", a=1), inside[:, :]).then_inc(w_ld["inside"], 16)
            sp.wait_ge(w_ld["inside"], 16)
            for tap in TAPS:
                sp.dma_start(inside_taps[tap:tap + 1, :],
                             mask_scratch[SHIFT[tap]:SHIFT[tap] + SL].rearrange("(a l) -> a l", a=1)
                             ).then_inc(dram_written, 16)
            sp.wait_ge(setup_pool, 1)
            for s, taps in enumerate(STACKS):
                nt = len(taps)
                for j, tap in enumerate(taps):
                    sp.dma_start(wconv[s][HC * j:HC * (j + 1), :, :], conv_w).then_inc(w_ld["conv"], 16)
                    sp.dma_start(wtap[s][HC * j:HC * (j + 1), :, :],
                                 conv_taps[tap].partition_broadcast(HC)).then_inc(w_ld["conv"], 16)
                sp.dma_start(wconv[s][HC * nt:HC * nt + nt, :, :],
                             conv_bias_row.partition_broadcast(nt)).then_inc(w_ld["conv"], 16)
                sp.dma_start(wtap[s][HC * nt:HC * nt + nt, :, :],
                             conv_taps[taps[0]:taps[0] + nt]).then_inc(w_ld["conv"], 16)
            sp.dma_start(wga_src[:, :], gate_w_a).then_inc(w_ld["gate"], 16)
            sp.dma_start(wgb_src[:, :], gate_w_b).then_inc(w_ld["gate"], 16)
            sp.dma_start(wqa_src[:, :], w_qkv_a).then_inc(w_ld["qkv"], 16)
            sp.dma_start(wqb_src[:, :], w_qkv_b).then_inc(w_ld["qkv"], 16)
            load_shift(sp)
            sp.dma_start(w1a_src[:, :], w1_a).then_inc(w_ld["w1a"], 16)
            sp.dma_start(w1b_src[:, :], w1_b).then_inc(w_ld["w1b"], 16)
            sp.dma_start(w2_src[:, :, :], w2).then_inc(w_ld["w2"], 16)
            store_padded(sp)
            sp.wait_ge(dram_written, 16 * len(TAPS))
            sp.wait_ge(w2_split, 1)
            for p in range(2):
                load_ring(sp, p)
            for p in range(2):
                sp.wait_ge(ring_ld[p], RING[p])
            for s in (x_ld, g_ld, b_ld):
                sp.wait_ge(s, 16)
            sp.wait_ge(setup_ready, 4)
            sp.sem_clear(per_image)
            sp.sem_inc(next_image, 1)

            with sp.Fori(0, B) as i:
                for h in range(NH):
                    if h in (2, 4):
                        p = 2 + (h - 2) // 2
                        sp.wait_ge(conv_ps, h)
                        load_ring(sp, p)
                    sp.wait_ge(conv_sb, h + 1)
                    if h == NH - 1:
                        sp.wait_ge(dram_written, i * (32 * QC) + 16 * len(TAPS))
                    sp.dma_start(vp[HC * (h % HPH):HC * (h % HPH + 1), h // HPH, :],
                                 qkve[h % 2][64:64 + HC, :]).then_inc(v_dma[h % 2], 16)
                def load_queries(j, first, end, signal):
                    for r, part in enumerate((QKh, QKl, QKh)):
                        sp.dma_start(QS[D * r:D * (r + 1), 2 * first + j:2 * end:2, :].bitcast(F32),
                                      part[D * j:D * (j + 1), first:end, :].bitcast(F32)).then_inc(signal, 16)

                def load_keys(j, first, end, signal):
                    for r, part in enumerate((QKh, QKh, QKl)):
                        sp.dma_start(KS[D * r:D * (r + 1), 2 * first + j:2 * end:2, :].bitcast(F32),
                                      part[64 + D * j:64 + D * (j + 1), first:end, :].bitcast(F32)).then_inc(signal, 16)

                def load_maxima(g, half):
                    sp.wait_ge(mrow_sb, QC * g + half + 1)
                    cols = slice(BANK * half, BANK * (half + 1))
                    for j, h in enumerate(GROUPS[g]):
                        sp.dma_start(QS[96:98, h, cols].bitcast(F32), mrow[g][2 * j:2 * j + 2, cols].bitcast(F32)
                                     ).then_inc(m_ld[g][half], 16)

                sp.wait_ge(qk_lo, QK_ORDER.index((0, 1)) + 1)
                for j in range(2):
                    load_queries(j, 0, 1, stack_ld[j])
                    load_keys(j, 0, 1, stack_ld[j])
                sp.wait_ge(qk_lo, 2 * len(GROUPS))
                for j in range(2):
                    load_queries(j, 1, len(GROUPS), stack_ld[2 + j])
                    load_keys(j, 1, len(GROUPS), stack_ld[2 + j])
                    if j == 0:
                        load_maxima(0, 0)
                for g, half, _ in DUE[1:]:
                    load_maxima(g, half)
                sp.wait_ge(o_ps, NC)
                load_image(sp, (i + 1) % B)
                sp.dma_start(b2_bc[:, :, :], b2.partition_broadcast(P)).then_inc(b2_ld, 16)
                load_shift(sp)
                store_padded(sp)
                sp.wait_ge(lnT_ps, 8)
                for p in range(2):
                    sp.wait_ge(ring_ld[p + 2], RING[p + 2])
                    load_ring(sp, p)

                def store_output(c):
                    o_img = out[i].rearrange("c a b -> c (a b)")
                    sp.dma_start(o_img[0:P, BANK * c:BANK * (c + 1)], outs_a[:, c, :]).then_inc(dram_written, 16)
                    sp.dma_start(o_img[P:C, BANK * c:BANK * (c + 1)], outs_b[:, c, :]).then_inc(dram_written, 16)

                sp.wait_ge(out_sb, 2)
                store_output(0)
                for p in range(2):
                    sp.wait_ge(ring_ld[p], RING[p])
                for s in (x_ld, g_ld, b_ld, b2_ld):
                    sp.wait_ge(s, 16)
                sp.wait_ge(out_sb, 4)
                sp.sem_clear(per_image)
                sp.sem_inc(next_image, 1)
                store_output(1)
            sp.wait_ge(dram_written, B * 32 * QC + 16 * len(TAPS))

        @block.gpsimd
        def _(pool):
            g = nc.gpsimd
            g.memset(wconv[0][:, :, :], 0.0)
            g.memset(wconv[1][:, :, :], 0.0)
            g.memset(wtap[0][:, :, :], 0.0)
            g.memset(wtap[1][:, :, :], 0.0).then_inc(setup_pool, 1)
            g.memset(inside[:, :], 0.0).then_inc(inside_zero, 1)
            pool.wait_ge(inside_zero, 1)
            g.memset(inside[:, 0:PW * (SH + 2)].rearrange("p (a b) -> p a b", b=PW)[:, 1:SH + 1, 1:SW + 1], 1.0
                     ).then_inc(setup_pool, 1)
            g.memset(minus_half[:, :], -0.5)
            g.memset(ones_avg[:, :], 1.0 / HALF)
            g.memset(ones32[:, :], 1.0)
            g.memset(before[:, :, :], 0.0)
            g.memset(block_mask[:, :], 0.0)
            g.memset(ident[:, :], 0.0)
            g.memset(ident_bf[:, :], 0.0)
            g.memset(keep_q[:, :], 0.0)
            g.memset(keep_k[:, :], 0.0).then_inc(setup_pool, 1)
            pool.wait_ge(setup_pool, 3)
            for m in (ident, ident_bf):
                g.affine_select(out=m[:, :], in_=m[:, :], compare_op=ALU.not_equal, fill=1.0, base=0,
                                pattern=[[-1, P]], channel_multiplier=1)
            g.affine_select(out=keep_q[:, :], in_=keep_q[:, :], compare_op=ALU.is_ge, fill=NEG, base=0,
                            pattern=[[-1, P]], channel_multiplier=1)
            g.affine_select(out=keep_k[:, :], in_=keep_k[:, :], compare_op=ALU.is_ge, fill=NEG, base=0,
                            pattern=[[1, P]], channel_multiplier=-1)
            g.affine_select(out=before[:, :, :], in_=before[:, :, :], compare_op=ALU.is_ge, fill=1.0, base=0,
                            pattern=[[-1, E], [1, E]], channel_multiplier=0)
            bm = block_mask[:, :].rearrange("p (h c) -> p h c", c=HC)
            g.affine_select(out=bm, in_=bm, compare_op=ALU.is_ge, fill=NEG, base=0,
                            pattern=[[-HC, HPH], [0, HC]], channel_multiplier=1).then_inc(setup_pool, 1)
            pool.wait_ge(setup_pool, 4)
            g.affine_select(out=bm, in_=bm, compare_op=ALU.is_ge, fill=NEG, base=HC - 1,
                            pattern=[[HC, HPH], [0, HC]], channel_multiplier=-1).then_inc(setup_pool, 1)
            image_rstd(pool)
            pad_image(pool)
            pool.wait_ge(padded, 2)
            pool.sem_inc(setup_ready, 1)

            with pool.Fori(0, B) as i:
                start_image(pool, i)

                def token_rstd(count):
                    pool.wait_ge(veps, count)
                    ch = slice(TPC * ((count - 1) % 2), TPC * ((count - 1) % 2 + 1))
                    g.tensor_tensor(rstd[:, 1, ch], rstd[:, 0, ch], minus_half[:, 0:TPC], ALU.pow).then_inc(rstd_sb, 1)

                token_rstd(1)
                token_rstd(2)
                pool.wait_ge(xhat_sb, NC)
                g.tensor_tensor(t_sb[:, :, :], t_sb[:, :, :],
                                b2p_bc[:, :].unsqueeze(1).to_broadcast([P, NC, C]), ALU.add).then_inc(tb_sb, 1)
                pool.wait_ge(tb_sb, 1)
                g.memset(KS[96:98, :, :].bitcast(F32), 1.0).then_inc(ks_ones, 1)
                token_rstd(3)
                token_rstd(4)
                image_rstd(pool)
                pad_image(pool)

        @block.vector
        def _(dve):
            v = nc.vector
            link = chained(dve)
            stats, partition_mean, deviation, variance, gain, shift = image_norm_steps(dve, link)
            for q in range(4):
                stats(q)
            partition_mean()
            dve.wait_ge(setup_pool, 5)
            v.tensor_copy(ident_r[:, :], ident[:, :]).then_inc(setup_dve, 1)
            deviation()
            dve.wait_ge(w_ld["proj"], 16 * 7)
            for k, rows in enumerate((P, CB)):
                v.tensor_copy(bp_row[0:rows, k, :], bp_src[0:rows, k:k + 1].to_broadcast([rows, P])
                              ).then_inc(setup_dve, 1)
            variance()
            for h in range(2):
                gain(h)
            dve.wait_ge(w_ld["small"], 16 * 6)
            link(v.reciprocal(ralpha[:, :], ralpha[:, :]))
            dve.wait_ge(setup_pe, 1)
            v.tensor_copy(w2pa[:, :], bank(0)[:, 0:C])
            v.tensor_copy(w2pb[:, :], bank(1)[0:CB, 0:C])
            link(v.tensor_tensor(b2p_bc[:, :], bank(3)[:, 0:C], bpb[:, :], ALU.add))
            dve.wait_ge(w_ld["conv"], 16 * (2 * len(TAPS) + 4))
            for s in range(2):
                link(v.tensor_tensor(wconv[s][:, :, :], wconv[s][:, :, :], wtap[s][:, :, :], ALU.mult))
            for h in range(2):
                shift(h)
            dve.wait_ge(w_ld["w2"], 16)
            link(v.tensor_copy(w2_parts[:, :, 0, :], w2_src[:, :, :]))
            v.tensor_tensor(w2_parts[:, :, 1, :], w2_src[:, :, :], w2_parts[:, :, 0, :].bitcast(F32), ALU.subtract
                            ).then_inc(w2_split, 1)
            for key, sets in (("gate", ((wga_hi, wga_lo, wga_src), (wgb_hi, wgb_lo, wgb_src))),
                              ("qkv", ((wqa_hi, wqa_lo, wqa_src), (wqb_hi, wqb_lo, wqb_src))),
                              ("w1a", ((w1a_hi, w1a_lo, w1a_src),)), ("w1b", ((w1b_hi, w1b_lo, w1b_src),))):
                dve.wait_ge(w_ld[key], 16 * len(sets))
                for hi, lo, src in sets:
                    full = tuple(slice(None) for _ in src.shape)
                    link(v.tensor_copy(hi[full], src[full]))
                    link(v.tensor_tensor(lo[full], src[full], hi[full].bitcast(F32), ALU.subtract))
            dve.wait_ge(xn_sb, 2)
            dve.wait_ge(setup_dve, 3)
            dve.sem_inc(setup_ready, 1)

            with dve.Fori(0, B) as i:
                start_image(dve, i)
                link = chained(dve)
                stats, partition_mean, deviation, variance, gain, shift = image_norm_steps(dve, link)
                def conv_qk(h):
                    dve.wait_ge(qkT_ps, h + 1)
                    src = bank(4 + h % 2).rearrange("p (k j c) -> p k j c", j=2, c=32)[:, :, :, 0:HC]
                    v.tensor_copy(qkt[:, :, :, HC * h:HC * (h + 1)], src).then_inc(qkT_sb, 1)

                def channel_logits(f):
                    dve.wait_ge(logit_ps, f + 1)
                    link(v.scalar_tensor_tensor(out=lm[:, f, :], in0=bank(6 + f)[0:HALF, 0:HALF],
                                                scalar=ralpha[:, f:f + 1], in1=block_mask[:, :],
                                                op0=ALU.mult, op1=ALU.add))
                    v.tensor_reduce(sm[:, f:f + 1], lm[:, f, :], AX, ALU.max, negate=True).then_inc(lm_sb, 1)

                def channel_attention(f):
                    dve.wait_ge(e_sb, f + 1)
                    link(v.reciprocal(sm[:, 4 + f:5 + f], sm[:, 2 + f:3 + f]))
                    v.tensor_scalar(lm[:, f, :], lm[:, f, :], sm[:, 4 + f:5 + f], None, ALU.mult).then_inc(attn_sb, 1)
                    dve.wait_ge(attnT_ps, f + 1)
                    v.tensor_copy(attn_t[:, f, :], bank(6 + f)[0:HALF, P:P + HALF]).then_inc(attnT_sb, 1)

                for h in range(NH):
                    conv_qk(h)
                    if h == HPH:
                        channel_logits(0)
                    if h == HPH + 1:
                        channel_attention(0)
                channel_logits(1)
                channel_attention(1)

                def token_stats(k, done, count):
                    dve.wait_ge(done, count)
                    ins = v.bn_stats(tstat[:, k, :], t_sb[:, k, :])
                    if k % TPC:
                        v.bn_aggr(tmv[:, k - 1, :], tstat[:, k - 1, :])
                    link(ins)
                    if k % TPC == TPC - 1:
                        link(v.bn_aggr(tmv[:, k, :], tstat[:, k, :]))
                        ch = slice(k - TPC + 1, k + 1)
                        v.tensor_scalar(rstd[:, 0, ch], tmv[:, ch, 1], 1e-5, None, ALU.add).then_inc(veps, 1)

                def normed(a, j):
                    dve.wait_ge(rstd_sb, 2 * a + j + 1)
                    for k in range(TPC * j, TPC * (j + 1)):
                        v.tensor_scalar(xhat[:, k, 0:C], t_sb[:, k, :], tmv[:, k, 0:1], rstd[:, 1, k:k + 1],
                                        ALU.subtract, ALU.mult)
                        v.tensor_scalar(xhat[:, k, C:2 * P], t_sb[:, k, P:C], tmv[:, k, 0:1], rstd[:, 1, k:k + 1],
                                        ALU.subtract, ALU.mult).then_inc(xhat_sb, 1)

                def low_channels(a, j):
                    cols = slice(BANK * j, BANK * (j + 1))
                    dve.wait_ge(T_hi, 4 * a + 2 * j + 1)
                    v.tensor_tensor(T2[:, cols], bank(4 + 2 * j), T0[:, cols].bitcast(F32), ALU.subtract
                                    ).then_inc(T_lo, 1)
                    dve.wait_ge(T_hi, 4 * a + 2 * j + 2)
                    v.tensor_tensor(T1[64:P, cols], bank(5 + 2 * j)[64:P, :], T1[64:P, cols].bitcast(F32),
                                    ALU.subtract).then_inc(T_lo, 1)

                def low_qk(n):
                    f, nh = QK_ORDER[n]
                    dve.wait_ge(qk_hi, n + 1)
                    v.tensor_tensor(QKl[:, f, BANK * nh:BANK * (nh + 1)], bank(n % 4),
                                    QKh[:, f, BANK * nh:BANK * (nh + 1)].bitcast(F32), ALU.subtract).then_inc(qk_lo, 1)

                def channel_mixed(k):
                    dve.wait_ge(y_ps, k + 1)
                    v.tensor_tensor(t_sb[:, k, :], bank(k % 4)[:, 0:C], bf_bc[:, :], ALU.add).then_inc(y_sb, 1)

                for k in range(NC):
                    channel_mixed(k)
                    if k:
                        token_stats(k - 1, y_sb, k)
                    if k == TPC + 2:
                        normed(0, 0)
                token_stats(NC - 1, y_sb, NC)
                low_channels(0, 0)
                normed(0, 1)
                for n in range(QK_FIRST):
                    low_qk(n)
                low_channels(0, 1)
                for n in range(QK_FIRST, 6):
                    low_qk(n)

                def score_max(n):
                    h, qc, k0, keys = PIECES[n]
                    dve.wait_ge(s_ps, n + 1)
                    dst = mx if k0 == 0 else mx_far
                    v.tensor_reduce(dst[:, qc, h:h + 1], bank(SLOT_BANK["scores", n])[:, 0:keys], AX, ALU.max
                                    ).then_inc(mx_sb, 1)

                def minus_max(g, half):
                    dve.wait_ge(mx_sb, DUE[QC * g + half][2])
                    src = mx[:, TPC * half:TPC * (half + 1), 2 * g:2 * g + 2]
                    dst = mneg[g][:, TPC * half:TPC * (half + 1), :, :]
                    if half:
                        link(v.tensor_tensor(src, src, mx_far[:, TPC:NC, 2 * g:2 * g + 2], ALU.max))
                    link(v.tensor_scalar(dst[:, :, :, 0], src, -1.0, None, ALU.mult))
                    v.scalar_tensor_tensor(out=dst[:, :, :, 1], in0=src, scalar=-1.0, in1=dst[:, :, :, 0].bitcast(F32),
                                           op0=ALU.mult, op1=ALU.subtract).then_inc(mneg_sb, 1)

                def maxima_of(uses):
                    for use in uses:
                        if use[0] == "scores":
                            score_max(use[1])
                            if use[1] in LAST_PIECE:
                                minus_max(*LAST_PIECE[use[1]])

                def quarter(n):
                    return slice(BANK // 4 * n, BANK // 4 * (n + 1))

                def reciprocals(g, n):
                    dve.wait_ge(unscaled_sb, QC * (g + 1))
                    link(v.reciprocal(sums[g][:, quarter(n)], sums[g][:, quarter(n)]))

                def scaled(g, c):
                    half = slice(64 * c, 64 * (c + 1))
                    v.tensor_tensor(aTa[64 * g:64 * (g + 1), BANK * c:BANK * (c + 1)], unscaled[g][half, :],
                                    sums[g][half, :], ALU.mult).then_inc(at_sb, 1)

                def last_scaled(c, n):
                    g = LAST_GROUP
                    dve.wait_ge(p_used, half_done(g, c))
                    dve.wait_ge(at_sb, AT_GROUP + TPC * c)
                    link(v.reciprocal(sums[0][0:64, quarter(n)], bank(6 + c)[64:P, quarter(n)]))
                    v.tensor_tensor(aTb[:, BANK * c + P * n:BANK * c + P * (n + 1)], bank(6 + c)[0:64, quarter(n)],
                                    sums[0][0:64, quarter(n)], ALU.mult).then_inc(at_sb, 1)

                maxima_of(PASS1_BEFORE)
                for s, (g, c, kb) in enumerate(STEPS):
                    sg = s % SG
                    maxima_of(PASS1_AT[s])
                    if g and 2 <= sg < 6:
                        reciprocals(g - 1, sg - 2)
                    if g and 6 <= sg < 8:
                        scaled(g - 1, sg - 6)
                for n in range(4):
                    last_scaled(0, n)
                def attended(k):
                    dve.wait_ge(o_ps, k + 1)
                    v.tensor_tensor(t_sb[:, k, :], bank(out_bank(k))[:, 0:C], t_sb[:, k, :], ALU.add).then_inc(o_sb, 1)

                dve.wait_ge(tb_sb, 1)
                for k in range(TPC):
                    attended(k)
                    if k:
                        token_stats(k - 1, o_sb, k)
                token_stats(TPC - 1, o_sb, TPC)
                last_scaled(1, 0)
                normed(1, 0)
                last_scaled(1, 1)
                low_channels(1, 0)
                for n in range(2, 4):
                    last_scaled(1, n)

                def attended_pair(k):
                    for kk in (k, k + 1):
                        attended(kk)
                    for kk in (k, k + 1):
                        token_stats(kk, o_sb, kk + 1)

                def onto_tokens(op, k, ins):
                    at = T_ORDER.index(op)
                    before_it = [n for n in range(at) if chunk_of(T_ORDER[n]) == k]
                    if before_it:
                        dve.wait_ge(t_acc, before_it[-1] + 1)
                    ins().then_inc(t_acc, 1)

                def chunk_of(op):
                    return op[1] // E if op[0] == "bias" else TPC * (op[1] // E) + op[2]

                def gating():
                    bc = lambda a: a.unsqueeze(2).to_broadcast([P, NC, E])
                    dve.wait_ge(gateT_ps, 1)
                    src = bank(6)[:, 0:NC * E].rearrange("p (k e) -> p k e", e=E)
                    link(v.tensor_tensor(gs[:, :, :], src, gb_bc[:, :].unsqueeze(1).to_broadcast([P, NC, E]), ALU.add))
                    link(v.tensor_reduce(gsum[:, :, 0], gs[:, :, :], AX, ALU.max))
                    v.tensor_tensor(gs[:, :, :], gs[:, :, :], bc(gsum[:, :, 0]), ALU.subtract).then_inc(gsub, 1)

                def routing():
                    dve.wait_ge(gexp_sb, 1)
                    other = gx[:, :, :].unsqueeze(2).to_broadcast([P, NC, E, E])
                    mine = gx[:, :, :].unsqueeze(3).to_broadcast([P, NC, E, E])
                    for e in range(E):
                        o, m = other[:, :, e, :], mine[:, :, e, :]
                        v.tensor_tensor(gcmp[:, :, e, :], o, m, ALU.is_gt)
                        last_eq = v.tensor_tensor(geq[:, :, e, :], o, m, ALU.is_equal)
                    link(last_eq)
                    for e in range(E):
                        last_eq = v.tensor_tensor(geq[:, :, e, :], geq[:, :, e, :],
                                                  before[:, e, :].unsqueeze(1).to_broadcast([P, NC, E]), ALU.mult)
                    link(last_eq)
                    link(v.tensor_tensor(gcmp[:, :, :, :], gcmp[:, :, :, :], geq[:, :, :, :], ALU.add))

                def gate_weights():
                    bc = lambda a: a.unsqueeze(2).to_broadcast([P, NC, E])
                    link(v.tensor_reduce(gs[:, :, :], gcmp[:, :, :, :], AX, ALU.add))
                    link(v.scalar_tensor_tensor(out=gate[:, :, :], in0=gs[:, :, :], scalar=1.5, in1=gx[:, :, :],
                                                op0=ALU.is_lt, op1=ALU.mult))
                    v.tensor_reduce(gsum[:, :, 1], gate[:, :, :], AX, ALU.add)
                    link(v.tensor_reduce(gsum[:, :, 2], gx[:, :, :], AX, ALU.add))
                    link(v.scalar_tensor_tensor(out=gsum[:, :, 3], in0=gsum[:, :, 2], scalar=1e-9, in1=gsum[:, :, 1],
                                                op0=ALU.mult, op1=ALU.add))
                    link(v.reciprocal(gsum[:, :, 1], gsum[:, :, 3]))
                    link(v.tensor_tensor(gate[:, :, :], gate[:, :, :], bc(gsum[:, :, 1]), ALU.mult))

                def low_part(n):
                    dve.wait_ge(gelu_sb, n + 1)
                    v.tensor_tensor(g_lo[:, n % 2, :], g32[:, n % 2, :], g_hi[:, n % 2, :].bitcast(F32),
                                    ALU.subtract).then_inc(lo_sb, 1)

                def bias_term(m):
                    k, e = m // E, m % E
                    if m == 0:
                        dve.wait_ge(b2_ld, 16)
                    onto_tokens(("bias", m), k, lambda: v.scalar_tensor_tensor(
                        out=t_sb[:, k, :], in0=b2_bc[:, e, :], scalar=gate[:, k, e:e + 1], in1=t_sb[:, k, :],
                        op0=ALU.mult, op1=ALU.add))

                def expert_sum(idx, pair):
                    c, e = idx // E, idx % E
                    if idx == QC * E - 1 and pair == 0:
                        dve.wait_ge(last_pair_ps, 1)
                    else:
                        dve.wait_ge(down_ps, J * (idx + 1))
                    for op in [op for op in T_ORDER if op[:2] == ("sum", idx) and op[2] // 2 == pair]:
                        tt, part = op[2:]
                        k = TPC * c + tt
                        src = bank(acc_bank(idx, tt))[:, C * part:C * (part + 1)]
                        onto_tokens(op, k, lambda: v.scalar_tensor_tensor(
                            out=t_sb[:, k, :], in0=src, scalar=gate[:, k, e:e + 1], in1=t_sb[:, k, :],
                            op0=ALU.mult, op1=ALU.add))

                image_steps = {8: lambda: stats(0), 9: lambda: stats(1), 10: lambda: stats(2),
                               11: lambda: (stats(3), partition_mean()), STAT + 1: deviation, STAT + 3: variance,
                               STAT + 4: lambda: gain(0), STAT + 7: lambda: gain(1),
                               STAT + 10: lambda: shift(0), STAT + 13: lambda: shift(1)}
                for n in range(NT):
                    low_part(n)
                    if n < 2:
                        attended_pair(TPC + 2 * n)
                    if n == 2:
                        normed(1, 1)
                    if n == 3:
                        low_channels(1, 1)
                    if n == 5:
                        gating()
                        routing()
                        gate_weights()
                    if n >= J and n % J < 2:
                        expert_sum(n // J - 1, n % J)
                    if BIAS0 <= n < BIAS0 + NC * E:
                        bias_term(n - BIAS0)
                    if n in image_steps:
                        image_steps[n]()
                for pair in range(2):
                    expert_sum(QC * E - 1, pair)

        @block.scalar
        def _(act):
            a = nc.scalar
            act.sem_inc(setup_ready, 1)

            with act.Fori(0, B) as i:
                start_image(act, i)
                def conv_out(h):
                    act.wait_ge(conv_ps, h + 1)
                    if h >= 2:
                        act.wait_ge(qkT_ps, h - 1)
                        act.wait_ge(v_dma[h % 2], 16 * (h // 2))
                    a.activation(qkve[h % 2][:, :], bank(2 * (h % 2), 2)[0:CM, :], ACT.Identity,
                                 bias=convb[:, h:h + 1]).then_inc(conv_sb, 1)

                def channel_exp(f):
                    act.wait_ge(lm_sb, f + 1)
                    a.activation(lm[:, f, :], lm[:, f, :], ACT.Exp, bias=sm[:, f:f + 1],
                                 accum_out=sm[:, 2 + f:3 + f]).then_inc(e_sb, 1)

                def mixing(f):
                    act.wait_ge(mix_ps, f + 1)
                    a.activation(mix[:, f, :], bank(6 + f)[0:HALF, 2 * P:2 * P + C], ACT.Copy).then_inc(mix_sb, 1)

                for h in range(NH):
                    conv_out(h)
                    if h == HPH + 1:
                        channel_exp(0)
                mixing(0)
                channel_exp(1)
                mixing(1)

                def high_channels(norm, j):
                    for b, dst in ((4 + 2 * j, T0), (5 + 2 * j, T1)):
                        act.wait_ge(lnT_ps, 4 * norm + b - 3)
                        a.activation(dst[:, BANK * j:BANK * (j + 1)], bank(b), ACT.Copy).then_inc(T_hi, 1)

                def values_out(k):
                    act.wait_ge(v_ps, k + 1)
                    a.activation(v_sb[:, k, :], bank(4 + k % 4)[:, 0:C], ACT.Copy).then_inc(v_done, 1)

                def maxima_row(g, half):
                    act.wait_ge(mT_ps, QC * g + half + 1)
                    a.activation(mrow[g][:, BANK * half:BANK * (half + 1)],
                                 bank(SLOT_BANK["maxima", g, half])[0:2 * len(GROUPS[g]), :], ACT.Copy
                                 ).then_inc(mrow_sb, 1)

                def half_out(g, c):
                    act.wait_ge(p_used, half_done(g, c))
                    half = slice(64 * c, 64 * (c + 1))
                    a.activation(unscaled[g][half, :], bank(6 + c)[0:64, :], ACT.Copy)
                    a.activation(sums[g][half, :], bank(6 + c)[64:P, :], ACT.Copy).then_inc(unscaled_sb, 1)

                high_channels(0, 0)
                for n in range(6):
                    if n == QK_FIRST:
                        high_channels(0, 1)
                    f, nh = QK_ORDER[n]
                    act.wait_ge(qk_ps, n + 1)
                    a.activation(QKh[:, f, BANK * nh:BANK * (nh + 1)], bank(n % 4), ACT.Copy).then_inc(qk_hi, 1)
                for k in range(NC):
                    values_out(k)
                for use in PASS1_BEFORE:
                    if use[0] == "maxima":
                        maxima_row(*use[1:])
                for signal in stack_ld:
                    act.wait_ge(signal, STACK_LOADS)
                for s, (g, c, kb) in enumerate(STEPS):
                    off, w = query_range(c, kb)
                    act.wait_ge(st_ps, s + 1)
                    if s >= 4:
                        act.wait_ge(p_used, s - 3)
                    a.activation(PT[:, 2 * (s % 4):2 * (s % 4) + 2, 0:w],
                                 bank(2 + 2 * (s % 2), 2).rearrange("p (h q) -> p h q", h=2)[:, :, 0:w],
                                 ACT.Exp, scale=SCALE).then_inc(p_sb, 1)
                    for use in PASS1_AT[s]:
                        if use[0] == "maxima":
                            maxima_row(*use[1:])
                    if g < LAST_GROUP and s % SG == TPC + 1:
                        half_out(g, 0)
                    if g and s % SG == 1:
                        half_out(g - 1, 1)
                high_channels(1, 0)

                def outputs(c):
                    for part, rows, dst in ((0, P, outs_a[:, c, :]), (1, CB, outs_b[:, c, :])):
                        act.wait_ge(outT_ps, 2 * c + part + 1)
                        a.activation(dst, bank(acc_bank(*out_use[2 * c + part]))[0:rows, :], ACT.Copy
                                     ).then_inc(out_sb, 1)

                def gate_rows():
                    for c in range(QC):
                        act.wait_ge(gate_ps, c + 1)
                        a.activation(grow[:, c, :], bank(6 + c)[0:E, :], ACT.Copy).then_inc(grow_sb, 1)

                def gate_exp():
                    act.wait_ge(gsub, 1)
                    a.activation(gx[:, :, :], gs[:, :, :], ACT.Exp).then_inc(gexp_sb, 1)

                for n in range(NT):
                    e, j = n // J % E, n % J
                    act.wait_ge(up_ps, n + 1)
                    if n >= 2:
                        act.wait_ge(down_ps, n - 1)
                        act.wait_ge(lo_sb, n - 1)
                    b1 = b1_sb[:, e * J + j:e * J + j + 1]
                    a.activation(g32[:, n % 2, :], bank(n % 2), ACT.Gelu, bias=b1)
                    a.activation(g_hi[:, n % 2, :], bank(n % 2), ACT.Gelu, bias=b1).then_inc(gelu_sb, 1)
                    if n == 3:
                        high_channels(1, 1)
                    if n == 5:
                        gate_rows()
                        gate_exp()
                    if n == OUT0 + 1:
                        outputs(0)
                outputs(1)

        @block.tensor
        def _(pe):
            t = nc.tensor

            pe.wait_ge(setup_pool, 5)
            average_mean(pe)
            average_var(pe)
            pe.wait_ge(w_ld["proj"], 16 * 7)
            pe.wait_ge(setup_dve, 3)
            wa, wb, wta, wtb = wp_src[0], wp_src[1][0:CB, :], wp_src[2], wp_src[3][0:CB, :]
            for b, rows, la, lb in ((0, P, wa[:, 0:P], wb[:, 0:P]), (1, CB, wa[:, P:C], wb[:, P:C]),
                                    (3, P, bp_row[:, 0, :], bp_row[0:CB, 1, :])):
                t.matmul(bank(b)[0:rows, 0:C], la, wta[:, :], start=True, stop=False)
                last = t.matmul(bank(b)[0:rows, 0:C], lb, wtb, start=False, stop=True)
            last.then_inc(setup_pe, 1)
            pe.sem_inc(setup_ready, 1)

            with pe.Fori(0, B) as i:
                start_image(pe, i)

                def conv(h):
                    p = h // 2
                    if p >= 2 and h % 2 == 0:
                        pe.wait_ge(ring_ld[p], RING[p])
                    if h >= 2:
                        pe.wait_ge(conv_sb, h - 1)
                    for nh in range(QC):
                        for s in range(2):
                            rhs = ring[p % 2][s][0:KROWS[s], h % 2, :].rearrange(
                                "p (a b) -> p a b", b=PW)[:, SH // QC * nh:SH // QC * (nh + 1), 0:SW]
                            last = t.matmul(bank(2 * (h % 2) + nh)[0:CM, :], wconv[s][0:KROWS[s], h, :], rhs,
                                            start=s == 0, stop=s == 1)
                    last.then_inc(conv_ps, 1)

                def conv_transposes(h):
                    pe.wait_ge(conv_sb, h + 1)
                    if h >= 2:
                        pe.wait_ge(qkT_sb, h - 1)
                    for k in range(NC):
                        last = t.transpose(bank(4 + h % 2)[:, 64 * k:64 * k + 56],
                                           qkve[h % 2][0:56, P * k:P * (k + 1)], ident[0:56, 0:56])
                    last.then_inc(qkT_ps, 1)

                def channel_products(f):
                    ch = slice(HALF * f, HALF * (f + 1))
                    pe.wait_ge(qkT_sb, HPH * (f + 1))
                    for k in range(NC):
                        last = t.matmul(bank(6 + f)[0:HALF, 0:HALF], qkt[:, k, 1, ch], qkt[:, k, 0, ch],
                                        start=k == 0, stop=k == NC - 1)
                    last.then_inc(logit_ps, 1)

                def attention_transpose(f):
                    pe.wait_ge(attn_sb, f + 1)
                    t.transpose(bank(6 + f)[0:HALF, P:P + HALF], lm[:, f, :], ident[0:HALF, 0:HALF]).then_inc(attnT_ps, 1)

                def mixing(f):
                    pe.wait_ge(attnT_sb, f + 1)
                    t.matmul(bank(6 + f)[0:HALF, 2 * P:2 * P + C], attn_t[:, f, :], wf_t[:, f, :],
                             start=True, stop=True).then_inc(mix_ps, 1)

                def input_and_first_heads(k):
                    o = bank(k % 4)
                    for f in range(2):
                        t.matmul(o[:, HALF * f:HALF * (f + 1)], xn[:, f, P * k:P * (k + 1)], ident[0:HALF, 0:HALF],
                                 start=f == 0, stop=False, skip_group_check=True)
                    t.matmul(o[:, 0:C], vp[:, 0, P * k:P * (k + 1)], mix[:, 0, :], start=False, stop=False,
                             skip_group_check=True)

                def last_heads(k):
                    t.matmul(bank(k % 4)[:, 0:C], vp[:, 1, P * k:P * (k + 1)], mix[:, 1, :], start=False, stop=True,
                             skip_group_check=True).then_inc(y_ps, 1)

                for h in range(NH):
                    conv(h)
                    if h:
                        conv_transposes(h - 1)
                    if h == HPH + 1:
                        channel_products(0)
                    if h == HPH + 2:
                        attention_transpose(0)
                    if h == HPH + 3:
                        mixing(0)
                conv_transposes(NH - 1)
                channel_products(1)
                pe.wait_ge(mix_sb, 1)
                for p in range(2):
                    pe.wait_ge(v_dma[p], 16 * NH // 2)
                for k in range(4):
                    input_and_first_heads(k)
                attention_transpose(1)
                mixing(1)
                pe.wait_ge(mix_sb, 2)
                for k in range(NC):
                    if k >= 4:
                        pe.wait_ge(y_sb, k - 3)
                        input_and_first_heads(k)
                    last_heads(k)

                def norm_transposes(norm, j):
                    pe.wait_ge(xhat_sb, NC * norm + TPC * (j + 1))
                    for b, c0 in ((4 + 2 * j, 0), (5 + 2 * j, P)):
                        for kk in range(TPC):
                            last = t.transpose(bank(b)[:, P * kk:P * (kk + 1)],
                                               xhat[:, TPC * j + kk, c0:c0 + P], ident[:, :])
                        last.then_inc(lnT_ps, 1)

                norm_transposes(0, 0)

                def parts(wa_hi, wa_lo, wb_hi, wb_lo):
                    return ((T0, wa_hi), (T0, wa_lo), (T2, wa_hi), (T1, wb_hi), (T1, wb_lo))

                qkv = parts(wqa_hi, wqa_lo, wqb_hi, wqb_lo)

                def queries_keys(n):
                    f, nh = QK_ORDER[n]
                    if f == 0:
                        pe.wait_ge(T_lo, 2 * (nh + 1))
                        pe.wait_ge(T_hi, 2 * (nh + 1))
                    if n >= 4:
                        pe.wait_ge(qk_lo, n - 3)
                    if n == 0:
                        pe.wait_ge(y_sb, NC)
                    for m, (act_part, w_part) in enumerate(qkv):
                        last = t.matmul(bank(n % 4), w_part[:, P * f:P * (f + 1)],
                                        act_part[:, BANK * nh:BANK * (nh + 1)], start=m == 0, stop=m == 4)
                    last.then_inc(qk_ps, 1)

                def values_of_tokens(k):
                    if k >= 4:
                        pe.wait_ge(v_done, k - 3)
                    for m, (act_part, w_part) in enumerate(qkv):
                        last = t.matmul(bank(4 + k % 4)[:, 0:C], act_part[:, P * k:P * (k + 1)],
                                        w_part[:, 2 * C:3 * C], start=m == 0, stop=m == 4)
                    last.then_inc(v_ps, 1)

                for n in range(QK_FIRST):
                    queries_keys(n)
                norm_transposes(0, 1)
                for n in range(QK_FIRST, 6):
                    queries_keys(n)
                for k in range(NC):
                    values_of_tokens(k)

                def bank_read(b, end):
                    uses = [use for use in SLOTS[:end] if SLOT_BANK[use] == b]
                    if uses:
                        kind, *n = uses[-1]
                        if kind == "scores":
                            pe.wait_ge(mx_sb, n[0] + 1)
                        else:
                            pe.wait_ge(mrow_sb, QC * n[0] + n[1] + 1)

                def query_scores(n):
                    h, qc, k0, keys = PIECES[n]
                    b = SLOT_BANK["scores", n]
                    if n == 0:
                        pe.wait_ge(qk_lo, 6)
                    if qc == 0 and h < len(stack_ld):
                        pe.wait_ge(stack_ld[h], STACK_LOADS)
                    bank_read(b, SLOTS.index(("scores", n)))
                    o = bank(b)
                    diagonal = k0 + keys == P * (qc + 1)
                    last = t.matmul(o[:, 0:keys], QS[0:96, h, P * qc:P * (qc + 1)], KS[0:96, h, k0:k0 + keys],
                                    start=True, stop=not diagonal, skip_group_check=True)
                    if diagonal:
                        last = t.matmul(o[:, keys - P:keys], ident_bf[:, :], keep_q[:, :], start=False, stop=True,
                                        skip_group_check=True)
                    last.then_inc(s_ps, 1)

                def transposed_maxima(g, half):
                    b = SLOT_BANK["maxima", g, half]
                    bank_read(b, SLOTS.index(("maxima", g, half)))
                    pe.wait_ge(mneg_sb, QC * g + half + 1)
                    for kk in range(TPC):
                        last = t.matmul(bank(b)[0:2 * len(GROUPS[g]), P * kk:P * (kk + 1)],
                                        mneg[g][:, TPC * half + kk, :, :].rearrange("p h r -> p (h r)"), ident_r[:, :],
                                        start=True, stop=True)
                    last.then_inc(mT_ps, 1)

                def pass1(uses):
                    for use in uses:
                        if use[0] == "scores":
                            query_scores(use[1])
                        else:
                            transposed_maxima(*use[1:])

                pass1(PASS1_BEFORE)
                pe.wait_ge(v_done, NC)
                pe.wait_ge(ks_ones, 1)

                def scores(s):
                    g, c, kb = STEPS[s]
                    off, w = query_range(c, kb)
                    if s >= 2:
                        pe.wait_ge(p_sb, s - 1)
                    if s == 0:
                        for b in (2, 3):
                            bank_read(b, len(PASS1_BEFORE))
                    if kb == 0:
                        pe.wait_ge(m_ld[g][c], 16 * len(GROUPS[g]))
                    diagonal = kb >= TPC * c
                    for j, h in enumerate(GROUPS[g]):
                        o = bank(2 + 2 * (s % 2) + j)
                        last = t.matmul(o[:, 0:w], KS[0:98, h, P * kb:P * (kb + 1)],
                                        QS[0:98, h, BANK * c + off:BANK * (c + 1)], start=True, stop=not diagonal,
                                        skip_group_check=True)
                        if diagonal:
                            last = t.matmul(o[:, 0:P], ident_bf[:, :], keep_k[:, :], start=False, stop=True,
                                            skip_group_check=True)
                    last.then_inc(st_ps, 1)

                def values(s):
                    g, c, kb = STEPS[s]
                    off, w = query_range(c, kb)
                    first, end = kb == 0, kb == TPC * (c + 1) - 1
                    if first and g:
                        pe.wait_ge(unscaled_sb, QC * (g - 1) + c + 1)
                    pe.wait_ge(p_sb, s + 1)
                    for row0, w_of in ((0, lambda h: v_sb[:, kb, D * h:D * (h + 1)]), (64, lambda h: ones32[:, :])):
                        for j, h in enumerate(GROUPS[g]):
                            last = t.matmul(bank(6 + c)[row0 + D * j:row0 + D * (j + 1), off:BANK], w_of(h),
                                            PT[:, 2 * (s % 4) + j, 0:w], start=first, stop=end,
                                            skip_group_check=True)
                    last.then_inc(p_used, 1)

                def output_projection(k):
                    pe.wait_ge(at_sb, AT_GROUP + (TPC if k < TPC else TPC + 1 if k == TPC else NC))
                    if k == 0:
                        pe.wait_ge(mrow_sb, QC * len(GROUPS))
                    if k % TPC >= 2:
                        pe.wait_ge(o_sb, k - 1)
                    o = bank(out_bank(k))[:, 0:C]
                    t.matmul(o, aTa[:, P * k:P * (k + 1)], w2pa[:, :], start=True, stop=False)
                    t.matmul(o, aTb[:, P * k:P * (k + 1)], w2pb[:, :], start=False, stop=True).then_inc(o_ps, 1)

                for s in range(len(STEPS) + 1):
                    if s < len(STEPS):
                        scores(s)
                        pass1(PASS1_AT[s])
                    if s:
                        values(s - 1)
                    if s in (OUT_STEP, OUT_STEP + 1):
                        for k in range(2 * (s - OUT_STEP), 2 * (s - OUT_STEP) + 2):
                            output_projection(k)
                norm_transposes(1, 0)

                def gate_scores():
                    for c in range(QC):
                        for m, (act_part, w_part) in enumerate(parts(wga_hi, wga_lo, wgb_hi, wgb_lo)):
                            last = t.matmul(bank(6 + c)[0:E, :], w_part[:, :], act_part[:, BANK * c:BANK * (c + 1)],
                                            start=m == 0, stop=m == 4)
                        last.then_inc(gate_ps, 1)

                def gate_transposes():
                    pe.wait_ge(grow_sb, QC)
                    for k in range(NC):
                        last = t.transpose(bank(6)[:, E * k:E * (k + 1)],
                                           grow[:, k // TPC, P * (k % TPC):P * (k % TPC + 1)], ident[0:E, 0:E])
                    last.then_inc(gateT_ps, 1)

                def up(n):
                    c, e, j = n // (E * J), n // J % E, n % J
                    if n >= 2:
                        pe.wait_ge(gelu_sb, n - 1)
                    for m, (act_part, w_part) in enumerate(parts(w1a_hi, w1a_lo, w1b_hi, w1b_lo)):
                        last = t.matmul(bank(n % 2), w_part[:, HID * e + P * j:HID * e + P * (j + 1)],
                                        act_part[:, BANK * c:BANK * (c + 1)], start=m == 0, stop=m == 4)
                    last.then_inc(up_ps, 1)

                def bank_free(idx, tt, sums=True):
                    pos = TPC * idx + tt - 6
                    if pos >= 0:
                        pe.wait_ge(t_acc, t_count("sum", pos // TPC, pos % TPC, 1))
                    if sums and (idx, tt) == stat_use:
                        pe.wait_ge(img_veps, 1)
                    if sums and (idx, tt) in out_use:
                        pe.wait_ge(out_sb, out_use.index((idx, tt)) + 1)

                def down(n, pairs):
                    idx, j = n // J, n % J
                    e = idx % E
                    if n == J:
                        pe.wait_ge(gsub, 1)
                    pe.wait_ge(gelu_sb, n + 1)
                    for pair in pairs:
                        for tt in (2 * pair, 2 * pair + 1):
                            if j == 0:
                                bank_free(idx, tt)
                            t.matmul(bank(acc_bank(idx, tt))[:, 0:2 * C], g_hi[:, n % 2, P * tt:P * (tt + 1)],
                                     w2_parts[:, e * J + j, :, :].rearrange("p r c -> p (r c)"),
                                     start=j == 0, stop=False, skip_group_check=True)
                        if pair == 0:
                            pe.wait_ge(lo_sb, n + 1)
                        for tt in (2 * pair, 2 * pair + 1):
                            last = t.matmul(bank(acc_bank(idx, tt))[:, 0:C], g_lo[:, n % 2, P * tt:P * (tt + 1)],
                                            w2_parts[:, e * J + j, 0, :], start=False, stop=j == J - 1,
                                            skip_group_check=True)
                        if n == NT - 1 and pair == 0:
                            last.then_inc(last_pair_ps, 1)
                    if pairs[-1] == 1:
                        last.then_inc(down_ps, 1)

                def out_transposes(c):
                    pe.wait_ge(t_acc, t_count("sum", E * (c + 1) - 1, TPC - 1, 1))
                    for part, c0, rows in ((0, 0, P), (1, P, CB)):
                        use = out_use[2 * c + part]
                        bank_free(*use, sums=False)
                        for kk in range(TPC):
                            last = t.transpose(bank(acc_bank(*use))[0:rows, P * kk:P * (kk + 1)],
                                               t_sb[:, TPC * c + kk, c0:c0 + rows], ident[:, :])
                        last.then_inc(outT_ps, 1)

                pe.wait_ge(T_lo, 6)
                pe.wait_ge(T_hi, 6)
                up(0)
                for n in range(NT):
                    if n == 5:
                        gate_transposes()
                    begins_pass = n >= J and n % J == 0
                    if n + 1 < NT and not (n > J and n % J == 1):
                        up(n + 1)
                    if n < 2:
                        for k in range(TPC + 2 * n, TPC + 2 * n + 2):
                            output_projection(k)
                    if n == 3:
                        norm_transposes(1, 1)
                    if n == 4:
                        pe.wait_ge(T_lo, 8)
                        pe.wait_ge(T_hi, 8)
                        gate_scores()
                    if begins_pass:
                        down(n, [0])
                        up(n + 2)
                        down(n, [1])
                    else:
                        down(n, [0, 1])
                    if n == STAT:
                        bank_free(*stat_use, sums=False)
                        average_mean(pe)
                    if n == STAT + 2:
                        average_var(pe)
                    if n == OUT0:
                        out_transposes(0)
                out_transposes(1)


def kernel(**inputs):
    import numpy as np
    import concourse.bacc as bacc
    from concourse.bass_utils import run_bass_kernel_spmd

    a = {k: np.asarray(v) for k, v in inputs.items()}
    f = np.float32
    nh, hc = a["L0_conv_bq_p"].shape
    kinds = "qkv"

    def per_kind(parts):
        pad = np.zeros(parts[0].shape[:-1] + (32 - hc,), f)
        return np.ascontiguousarray(np.concatenate([parts[0], pad, parts[1], pad, parts[2]], axis=-1))

    conv_w = per_kind([a[f"L0_conv_w{k}_p"].transpose(2, 0, 1) for k in kinds])
    conv_bias_row = per_kind([a[f"L0_conv_b{k}_p"] for k in kinds])
    conv_taps = per_kind([a[f"L0_conv_w{k}_d"].reshape(nh, hc, 9).transpose(2, 0, 1) for k in kinds])
    conv_bias = np.ascontiguousarray(per_kind([a[f"L0_conv_b{k}_d"].reshape(nh, hc) for k in kinds]).T)
    alpha_rows = np.ascontiguousarray(np.repeat(a["L0_conv_alpha"], hc).reshape(2, -1).T)
    w = a["L1_attn_W_qkv"].reshape(6, 3, -1, a["L1_attn_W_qkv"].shape[1])
    c = w.shape[-1]
    k_, q_, v_ = (w[:, n].reshape(-1, c) for n in range(3))
    w_qkv = np.concatenate([part[64 * g:64 * (g + 1)] for g in range(3) for part in (q_, k_)] + [v_]).T

    def ab(m):
        return np.ascontiguousarray(m[:128]), np.ascontiguousarray(np.concatenate([m[128:], m[128:]]))

    w_qkv_a, w_qkv_b = ab(w_qkv)
    gate_a, gate_b2 = ab(a["L1_ffn_gate_w"])
    w1_a, w1_b = ab(a["L1_ffn_w1"].transpose(1, 0, 2).reshape(c, -1))
    e, hid, _ = a["L1_ffn_w2"].shape
    arrays = {
        "x": a["x"], "ln_g": a["L0_conv_ln_g"], "ln_b": a["L0_conv_ln_b"],
        "conv_w": conv_w, "conv_bias_row": conv_bias_row, "conv_taps": conv_taps, "conv_bias": conv_bias,
        "alpha_rows": alpha_rows, "w_f_t": a["L0_conv_w_f"].T, "b_f": a["L0_conv_b_f"],
        "w_qkv_a": w_qkv_a, "w_qkv_b": w_qkv_b,
        "w_proj": a["L1_attn_W_proj"], "w_proj_t": a["L1_attn_W_proj"].T, "b_proj": a["L1_attn_b_proj"],
        "gate_w_a": gate_a, "gate_w_b": gate_b2, "gate_b": a["L1_ffn_gate_b"],
        "w1_a": w1_a, "w1_b": w1_b, "b1_t": a["L1_ffn_b1"].reshape(e * hid // 128, 128).T,
        "w2": a["L1_ffn_w2"].reshape(e * hid // 128, 128, c).transpose(1, 0, 2), "b2": a["L1_ffn_b2"],
    }
    arrays = {k: np.ascontiguousarray(v) for k, v in arrays.items()}
    nc = bacc.Bacc("TRN2", target_bir_lowering=False, num_devices=1, dynamic_dma_scratch_size=1024)
    aps = [nc.dram_tensor(k, v.shape, mybir.dt.from_np(v.dtype), kind="ExternalInput").ap() for k, v in arrays.items()]
    out = nc.dram_tensor("out", a["x"].shape, F32, kind="ExternalOutput").ap()
    hybrid_block_kernel(nc, *aps, out)
    r = run_bass_kernel_spmd(nc, [arrays], core_ids=[0])
    return r.results[0]["out"]
```
